# Optimizing a Trainium2 kernel written in Bass

```python
import numpy as np
import jax
import jax.numpy as jnp

def _softmax(x, axis=-1):
    return jax.nn.softmax(x, axis=axis)

def _gelu(x):
    return jax.nn.gelu(x, approximate=True)

def _silu(x):
    return jax.nn.silu(x)

def _sigmoid(x):
    return jax.nn.sigmoid(x)

def _layernorm(x, axis=-1, eps=1e-05):
    m = jnp.mean(x, axis=axis, keepdims=True)
    v = jnp.var(x, axis=axis, keepdims=True)
    return (x - m) / jnp.sqrt(v + eps)

def _scatter_add(tgt, idx, src, axis=0):
    return tgt.at[idx].add(src)

def _segment_sum(src, seg, n):
    return jax.ops.segment_sum(src, seg, n)
kernel_name = 'mk_conv_preact_d2_conv_nchw256_r2_2bc0f0'

def setup_inputs(seed: int=0):
    np.random.seed(seed)
    _w = jnp.asarray

    def _rec_inputs():
        import jax
        import jax.numpy as jnp
        _gk = jax.random.key(seed)
        x = -7.109e-05 + 0.9999 * jax.random.normal(jax.random.fold_in(_gk, 1), (16, 128, 64, 64), jnp.float32)
        return x
    x = _rec_inputs()

    def _L0_conv_setup():
        import jax, jax.numpy as jnp
        import numpy as np
        POS_IDX = np.array([0, 2, 4, 10, 14, 20, 22, 24])
        NEG_IDX = np.array([6, 7, 8, 11, 13, 16, 17, 18])

        def _build_rpdc_kernel(weight):
            C = weight.shape[0]
            w = weight.reshape(C, 1, 9)
            tap = w[:, :, 1:]
            buf = jnp.zeros((C, 1, 25), dtype=weight.dtype)
            buf = buf.at[:, :, POS_IDX].set(tap)
            buf = buf.at[:, :, NEG_IDX].set(-tap)
            return buf.reshape(C, 1, 5, 5)
        key = jax.random.key(seed)
        kx, kw = jax.random.split(key)
        x = jax.random.normal(kx, (16, 128, 64, 64), dtype=jnp.float32)
        weight = jax.random.normal(kw, (128, 1, 3, 3), dtype=jnp.float32) * 0.1
        return {'x': x, 'weight': weight}
    _L0_conv_all = _L0_conv_setup()
    _L0_conv_in = {k: v for k, v in _L0_conv_all.items() if k in ('weight',)}
    del _L0_conv_all

    def _L1_conv_setup():
        import jax, jax.numpy as jnp
        import numpy as np
        B, C, H, W = (16, 128, 64, 64)

        def make_rota_matrix(n_pos, channels):
            c = jnp.arange(channels)
            theta = 10000.0 ** (-2.0 * (c // 2).astype(jnp.float32) / channels)
            ang = jnp.arange(n_pos, dtype=jnp.float32)[:, None] * theta[None, :]
            cos_v = jnp.cos(ang)
            sign = jnp.where(c % 2 == 0, 1.0, -1.0)
            sin_v = jnp.sin(ang) * sign[None, :]
            sin_pos = c + jnp.where(c % 2 == 0, 1, -1)
            R = jnp.zeros((n_pos, channels, channels), dtype=jnp.float32)
            R = R.at[:, c, c].set(cos_v)
            R = R.at[:, sin_pos, c].set(sin_v)
            return R
        key = jax.random.key(seed)
        feats = jax.random.normal(key, (B, C, H, W), dtype=jnp.float32)
        rota_matrix = make_rota_matrix(H, C)
        return {'feats': feats, 'rota_matrix': rota_matrix}
    _L1_conv_all = _L1_conv_setup()
    _L1_conv_in = {k: v for k, v in _L1_conv_all.items() if k in ('rota_matrix',)}
    del _L1_conv_all
    return {'x': x, 'L0_conv_weight': _L0_conv_in['weight'], 'L1_conv_rota_matrix': _L1_conv_in['rota_matrix']}

def reference(x, L0_conv_weight, L1_conv_rota_matrix):
    import jax
    import jax.numpy as jnp

    def _L0_conv_ref(x, weight):
        import jax, jax.numpy as jnp
        import numpy as np
        POS_IDX = np.array([0, 2, 4, 10, 14, 20, 22, 24])
        NEG_IDX = np.array([6, 7, 8, 11, 13, 16, 17, 18])

        def _build_rpdc_kernel(weight):
            C = weight.shape[0]
            w = weight.reshape(C, 1, 9)
            tap = w[:, :, 1:]
            buf = jnp.zeros((C, 1, 25), dtype=weight.dtype)
            buf = buf.at[:, :, POS_IDX].set(tap)
            buf = buf.at[:, :, NEG_IDX].set(-tap)
            return buf.reshape(C, 1, 5, 5)
        C = weight.shape[0]
        kernel = _build_rpdc_kernel(weight)
        return jax.lax.conv_general_dilated(x, kernel, window_strides=(1, 1), padding=[(2, 2), (2, 2)], rhs_dilation=(1, 1), dimension_numbers=('NCHW', 'OIHW', 'NCHW'), feature_group_count=C)

    def _L1_conv_ref(feats, rota_matrix):
        import jax, jax.numpy as jnp
        import numpy as np
        B, C, H, W = (16, 128, 64, 64)

        def make_rota_matrix(n_pos, channels):
            c = jnp.arange(channels)
            theta = 10000.0 ** (-2.0 * (c // 2).astype(jnp.float32) / channels)
            ang = jnp.arange(n_pos, dtype=jnp.float32)[:, None] * theta[None, :]
            cos_v = jnp.cos(ang)
            sign = jnp.where(c % 2 == 0, 1.0, -1.0)
            sin_v = jnp.sin(ang) * sign[None, :]
            sin_pos = c + jnp.where(c % 2 == 0, 1, -1)
            R = jnp.zeros((n_pos, channels, channels), dtype=jnp.float32)
            R = R.at[:, c, c].set(cos_v)
            R = R.at[:, sin_pos, c].set(sin_v)
            return R
        R = rota_matrix[:feats.shape[2]]
        return jnp.einsum('hvc,bchw->bvhw', R, feats)

    def _gn(v, G=32, eps=1e-05):
        B_, C_, H_, W_ = v.shape
        g = v.reshape(B_, G, C_ // G, H_, W_)
        m = jnp.mean(g, axis=(2, 3, 4), keepdims=True)
        s = jnp.var(g, axis=(2, 3, 4), keepdims=True)
        return ((g - m) / jnp.sqrt(s + eps)).reshape(v.shape)

    def _ln_c(v, eps=1e-06):
        m = jnp.mean(v, axis=1, keepdims=True)
        s = jnp.var(v, axis=1, keepdims=True)
        return (v - m) / jnp.sqrt(s + eps)

    def _ln_t(v, eps=1e-05):
        m = jnp.mean(v, axis=-1, keepdims=True)
        s = jnp.var(v, axis=-1, keepdims=True)
        return (v - m) / jnp.sqrt(s + eps)

    def _to_tokens(v):
        B_, C_, H_, W_ = v.shape
        return v.reshape(B_, C_, H_ * W_).transpose(0, 2, 1)

    def _from_tokens(t, like):
        B_, C_, H_, W_ = like.shape
        return t.transpose(0, 2, 1).reshape(B_, C_, H_, W_)
    x = x + _L0_conv_ref(_gn(x), L0_conv_weight)
    x = x + _L1_conv_ref(_gn(x), L1_conv_rota_matrix)
    return x

_drawn_inputs = setup_inputs


def setup_inputs(seed=0):
    import zlib

    import numpy as np

    out = dict(_drawn_inputs(seed))
    spreads = {}
    factors = {}
    for name, (base, spread) in spreads.items():
        noise = np.random.default_rng([zlib.crc32(name.encode()), seed]).standard_normal(out[name].shape)
        drawn = base * np.exp(spread * noise) if base else spread * noise
        out[name] = jnp.asarray(drawn.astype(out[name].dtype))
    for name, factor in factors.items():
        out[name] = (out[name] * factor).astype(out[name].dtype)
    return out
```

```python
from contextlib import ExitStack

import concourse.bass as bass
from concourse import mybir

F32 = mybir.dt.float32
F32R = mybir.dt.float32r
ALU = mybir.AluOpType
ACT = mybir.ActivationFunctionType

P = 128
B, C, H, W = 16, 128, 64, 64
GC = 4
GROUPS = C // GC
ROWS = P // W
CHUNKS = H // ROWS
Q = 4
QB = B // Q
EPS = 1e-5

PITCH = W + 2
SLOT_MID = W - 1
WINDOW = 6 * PITCH
LINE = 528
KH = KW = 5
POS_IDX = (0, 2, 4, 10, 14, 20, 22, 24)
NEG_IDX = (6, 7, 8, 11, 13, 16, 17, 18)

LEAD = 2
XRING = 6
UNROLL = 6
FIRST_STEP, LAST_STEP = -3, GROUPS + 1
LOOP_START, LOOP_TRIPS = 4, 4

UCH = 2
RH = UCH * ROWS
BH = B // 2
UNITS = CHUNKS // UCH
GCOLS = UCH * BH * P
GRING = 8
AHEAD = 6
UUNROLL = GRING // 2
ULOOP_START, ULOOP_TRIPS = UUNROLL, UNITS // UUNROLL - 2


class Step:

    def __init__(self, at, res):
        self.at, self.res = at, res

    def __add__(self, n):
        return Step(self.at + n, self.res + n)

    def ring(self, n):
        return self.res % n

    def landings(self, n, each=16):
        return (self.at - self.ring(n)) * (each // n) + each

    def of(self, ap):
        if isinstance(self.at, int):
            return ap[self.at]
        part = ap[bass.ds(self.at, 1)]
        names = " ".join("abcdefg"[:len(part.shape) - 2])
        return part.rearrange(f"o p {names} -> (o p) {names}")


def conv_rotate_kernel(nc, x, weight, rota, out):
    tap_lines = nc.dram_tensor("tap_lines", (C, LINE), F32, kind="Internal").ap()
    x1_dram = nc.dram_tensor("x1_scratch", (C, CHUNKS, B, P), F32, kind="Internal").ap()
    norm2_dram = nc.dram_tensor("norm2_scratch", (C, 2 * B), F32, kind="Internal").ap()

    x_src = x.rearrange("b (g c) (i r) w -> g (c i) b (r w)", c=GC, r=ROWS)
    x1_dst = x1_dram.rearrange("(g c) i b e -> g (c i) (b e)", c=GC)
    norm2_dst = norm2_dram.rearrange("(g c) k -> g c k", c=GC)
    x1_src = [x1_dram[:, :, n * BH:(n + 1) * BH, :].rearrange("c (u i) b e -> u c i (b e)", i=UCH) for n in range(2)]
    out_dst = [[out[n * BH:(n + 1) * BH].rearrange("b c (u i r) w -> u i c b (r w)", i=UCH, r=ROWS)[:, i]
                for i in range(UCH)] for n in range(2)]
    rota_src = rota.rearrange("(u h) v c -> u v h c", h=RH)

    with ExitStack() as ctx:
        def sb(name, shape, dt=F32):
            return ctx.enter_context(nc.sbuf_tensor(name, shape, dt))

        def sem(name):
            return ctx.enter_context(nc.semaphore(name))

        tiles = sb("tiles", [P, GRING, B * P])
        g = sb("g", [P, B, P])
        high = sb("high", [P, 2, B, GC, CHUNKS + 2], F32R)
        low = sb("low", [P, 2, B, GC, CHUNKS + 2], F32R)
        y = sb("y", [P, 2, B, GC, CHUNKS])
        taps_raw = sb("taps_raw", [P, 2, GC, 6, PITCH])
        taps_hi = sb("taps_hi", [P, 2, GC, 6, W], F32R)
        taps_lo = sb("taps_lo", [P, 2, GC, 6, W], F32R)
        line = sb("line", [C, LINE])
        w_sb = sb("w_sb", [C, 9])
        ident = sb("ident", [P, P])
        ones_half = sb("ones_half", [P, P])
        ones_all = sb("ones_all", [P, P])
        eps = sb("eps", [P, 1])
        carrier = sb("carrier", [P, Q])
        stats = sb("stats", [P, 2, 2, B, 6])
        dev = sb("dev", [P, 2 * B, 2])
        dev2 = sb("dev2", [P, 2 * B, 2])
        std = sb("std", [P, 2, B])
        affine = sb("affine", [P, 2, 2, 2, B])
        norm2 = sb("norm2", [C, 2, B])

        ps = ctx.enter_context(nc.psum_tensor("ps", [P, 8, 512], F32))
        ps_turn = ps[:, 0:2, :]
        ps_conv = ps[:, 2:4, :]
        ps_back = ps[:, 4:6, :]
        ps_mean = ps[:, 6, 0:2 * B]
        ps_var = ps[:, 7, 0:2 * B]

        def flat(t, n, cols):
            return t[:, n].rearrange("p a b c -> p (a b c)")[:, 0:cols]

        gn = [flat(y, n, GCOLS) for n in range(2)]
        gn_hi = [flat(high, n, GCOLS) for n in range(2)]
        gn_lo = [flat(low, n, GCOLS) for n in range(2)]
        rot_raw = [flat(taps_raw, n, RH * C) for n in range(2)]
        rot_hi = [flat(taps_hi, n, RH * C) for n in range(2)]
        rot_lo = [flat(taps_lo, n, RH * C) for n in range(2)]

        w_landed = sem("w_landed")
        line_zeroed = sem("line_zeroed")
        line_ready = sem("line_ready")
        line_stored = sem("line_stored")
        ident_zeroed = sem("ident_zeroed")
        consts_ready = sem("consts_ready")
        x_landed = [sem(f"x_landed{n}") for n in range(2)]
        taps_landed = [sem(f"taps_landed{n}") for n in range(2)]
        taps_rounded = sem("taps_rounded")
        taps_split = sem("taps_split")
        stats_ready = sem("stats_ready")
        mean_ready = sem("mean_ready")
        dev_ready = sem("dev_ready")
        dev2_ready = sem("dev2_ready")
        var_ready = sem("var_ready")
        std_ready = sem("std_ready")
        scale_ready = sem("scale_ready")
        affine_ready = sem("affine_ready")
        normed = sem("normed")
        turned = sem("turned")
        high_ready = sem("high_ready")
        low_ready = sem("low_ready")
        convolved = sem("convolved")
        y_ready = sem("y_ready")
        turned_back = sem("turned_back")
        x1_ready = sem("x1_ready")
        x1_stored = [sem(f"x1_stored{n}") for n in range(2)]
        norm2_stored = [sem(f"norm2_stored{n}") for n in range(2)]
        norm2_landed = sem("norm2_landed")
        x1_landed = [sem(f"x1_landed{n}") for n in range(GRING)]
        rot_landed = [sem(f"rot_landed{n}") for n in range(2)]
        rot_turned = sem("rot_turned")
        rot_high = sem("rot_high")
        rot_split = sem("rot_split")
        gn_ready = sem("gn_ready")
        gn_high = sem("gn_high")
        gn_split = sem("gn_split")
        rotated = sem("rotated")
        out_ready = sem("out_ready")
        out_stored = [sem(f"out_stored{n}") for n in range(GRING)]

        block = ctx.enter_context(nc.Block())

        def has(s, shift):
            return 0 <= s.res + shift < GROUPS

        def norms(s):
            return 0 if has(s, 2) else 1, 2 if has(s, -2) else 1

        def finishes_norms(s):
            return has(s, 2) or has(s, -2)

        def stage1(engine, step):
            for s in range(FIRST_STEP, LOOP_START):
                step(Step(s, s))
            with engine.Fori(0, LOOP_TRIPS) as trip:
                for t in range(UNROLL):
                    step(Step(trip * UNROLL + (LOOP_START + t), LOOP_START + t))
            for s in range(LOOP_START + LOOP_TRIPS * UNROLL, LAST_STEP + 1):
                step(Step(s, s))

        def stage2(engine, unit):
            for u in range(ULOOP_START):
                unit(Step(u, u))
            with engine.Fori(0, ULOOP_TRIPS) as trip:
                for t in range(UUNROLL):
                    unit(Step(trip * UUNROLL + (ULOOP_START + t), ULOOP_START + t))
            for u in range(UNITS - UUNROLL, UNITS):
                unit(Step(u, u))

        def granule(u, half):
            return Step(u.at * 2 + half, u.res * 2 + half)

        @block.sync
        def _(sp):
            sp.dma_start(w_sb[:], weight.rearrange("c o a b -> c (o a b)")).then_inc(w_landed, 16)

            def load(k):
                par = k.ring(2)
                if k.res >= 2:
                    sp.wait_ge(x_landed[par], k.landings(2, 32) - 32)
                x_slot = tiles[:, k.ring(XRING), :].rearrange("p (b e) -> p b e", b=B)
                for half in (slice(0, BH), slice(BH, B)):
                    sp.dma_start(x_slot[:, half], k.of(x_src)[:, half]).then_inc(x_landed[par], 16)

            def load_taps(k):
                par = k.ring(2)
                if k.res >= 2:
                    sp.wait_ge(taps_split, k.at - 1)
                for r in range(ROWS):
                    window = bass.AP(tensor=tap_lines.tensor, offset=k.at * (GC * LINE) + r * PITCH,
                                     ap=[[1, W], [LINE, GC], [1, WINDOW]])
                    sp.dma_start(taps_raw[r * W:(r + 1) * W, par].rearrange("p c s w -> p c (s w)"),
                                 window).then_inc(taps_landed[par], 16)

            for k in range(2):
                load(Step(k, k))
            sp.wait_ge(line_ready, len(POS_IDX + NEG_IDX))
            sp.dma_start(tap_lines, line[:]).then_inc(line_stored, 16)
            sp.wait_ge(line_stored, 16)
            for k in range(2):
                load_taps(Step(k, k))
            for k in range(2, XRING):
                load(Step(k, k))

            def step(s):
                if s.res >= 0 and has(s, 2):
                    load_taps(s + 2)
                if has(s, -2) and has(s, XRING - 2):
                    sp.wait_ge(x1_ready, (s.at - 1) * Q)
                    load(s + (XRING - 2))
                if has(s, -2):
                    k = s + -2
                    sp.wait_ge(affine_ready, s.at + 3)
                    sp.dma_start(k.of(norm2_dst), affine[0:GC, s.ring(2), 1].rearrange("p a b -> p (a b)")
                                 ).then_inc(norm2_stored[k.ring(2)], 16)
                if has(s, -1):
                    k = s + -1
                    sp.wait_ge(x1_ready, k.at * Q + Q)
                    sp.dma_start(k.of(x1_dst), tiles[:, XRING + k.ring(2), :]
                                 ).then_inc(x1_stored[k.ring(2)], 16)

            stage1(sp, step)

            for n in range(2):
                sp.wait_ge(x1_stored[n], 16 * (GROUPS // 2))
                sp.wait_ge(norm2_stored[n], 16 * (GROUPS // 2))
            sp.dma_start(norm2[:], norm2_dram.rearrange("c (a b) -> c a b", a=2)).then_inc(norm2_landed, 16)

            def load_granule(u, half):
                n = granule(u, half)
                slot = n.ring(GRING)
                if n.res >= GRING:
                    sp.wait_ge(out_stored[slot], n.landings(GRING, 16 * UCH) - 16 * UCH)
                sp.dma_start(tiles[:, slot, :].rearrange("p (i f) -> p i f", i=UCH), u.of(x1_src[half])
                             ).then_inc(x1_landed[slot], 16)

            def load_rotations(u):
                if u.res >= 2:
                    sp.wait_ge(rot_turned, u.at - 1)
                sp.dma_start(rot_raw[u.ring(2)].rearrange("v (h c) -> v h c", h=RH), u.of(rota_src)
                             ).then_inc(rot_landed[u.ring(2)], 16)

            def store_granule(u, half):
                n = granule(u, half)
                slot = n.ring(GRING)
                sp.wait_ge(out_ready, n.at * RH + RH)
                for i in range(UCH):
                    sp.dma_start(u.of(out_dst[half][i]),
                                 tiles[:, slot, :].rearrange("p (i b e) -> p i b e", i=UCH, b=BH)[:, i]
                                 ).then_inc(out_stored[slot], 16)

            for u in range(AHEAD // 2):
                if u < 2:
                    load_rotations(Step(u, u))
                for half in range(2):
                    load_granule(Step(u, u), half)

            def unit(u):
                for half in range(2):
                    store_granule(u, half)
                    if u.res + AHEAD // 2 < UNITS:
                        load_granule(u + AHEAD // 2, half)
                if u.res + 2 < UNITS:
                    load_rotations(u + 2)

            stage2(sp, unit)
            for slot in range(GRING):
                sp.wait_ge(out_stored[slot], 16 * UCH * (2 * UNITS // GRING))

        @block.gpsimd
        def _(pool):
            nc.gpsimd.memset(ident[:], 0.0).then_inc(ident_zeroed, 1)
            nc.gpsimd.memset(ones_half[:], 1.0 / (2 * P)).then_inc(consts_ready, 1)
            nc.gpsimd.memset(ones_all[:], 1.0 / (P * P)).then_inc(consts_ready, 1)
            nc.gpsimd.memset(eps[:], EPS).then_inc(consts_ready, 1)
            pool.wait_ge(ident_zeroed, 1)
            nc.gpsimd.affine_select(out=ident[:], in_=ident[:], compare_op=ALU.not_equal, fill=1.0, base=0,
                                    pattern=[[-1, P]], channel_multiplier=1).then_inc(consts_ready, 1)
            for t in (high, low):
                for n in range(2):
                    for end in (0, CHUNKS + 1):
                        nc.gpsimd.memset(t[:, n, :, :, end:end + 1].bitcast(F32), 0.0).then_inc(consts_ready, 1)

            pool.wait_ge(consts_ready, 4)

            def normalise(k, q):
                pool.wait_ge(affine_ready, k.at + 1)
                if k.res >= 1:
                    pool.wait_ge(turned, (k.at - 1) * Q + q + 1)
                nc.gpsimd.tensor_tensor(carrier[:, q:q + 1], eps[:], eps[:], ALU.mult)
                for b in range(q * QB, (q + 1) * QB):
                    last = nc.gpsimd.tensor_scalar(g[:, b, :], tiles[:, k.ring(XRING), b * P:(b + 1) * P],
                                                   affine[:, k.ring(2), 0, 0, b:b + 1],
                                                   affine[:, k.ring(2), 0, 1, b:b + 1], ALU.mult, ALU.add)
                last.then_inc(normed, 1)

            def split_taps(k):
                par = k.ring(2)
                pool.wait_ge(taps_rounded, k.at + 1)
                nc.gpsimd.tensor_tensor(taps_lo[:, par], taps_raw[:, par, :, ::-1, W - 1::-1],
                                        taps_hi[:, par].bitcast(F32), ALU.subtract).then_inc(taps_split, 1)

            def step(s):
                for q in range(Q):
                    if q < Q - LEAD:
                        if has(s, 1):
                            normalise(s + 1, q + LEAD)
                            if q == Q - LEAD - 1:
                                split_taps(s + 1)
                    elif has(s, 2):
                        normalise(s + 2, q + LEAD - Q)

            stage1(pool, step)

            def unit(u):
                for half in range(2):
                    n = granule(u, half)
                    buf = n.ring(2)
                    pool.wait_ge(gn_high, n.at + 1)
                    if n.res >= 2:
                        pool.wait_ge(rotated, (n.at - 1) * RH)
                    nc.gpsimd.tensor_tensor(gn_lo[buf], gn[buf], gn_hi[buf].bitcast(F32),
                                            ALU.subtract).then_inc(gn_split, 1)

            stage2(pool, unit)

        @block.scalar
        def _(act):
            act.wait_ge(consts_ready, 4)

            def round_taps(k):
                par = k.ring(2)
                act.wait_ge(taps_landed[par], k.landings(2, 16 * ROWS))
                if k.res >= 2:
                    act.wait_ge(convolved, (k.at - 1) * GC)
                nc.scalar.activation(taps_hi[:, par], taps_raw[:, par, :, ::-1, W - 1::-1],
                                     ACT.Identity).then_inc(taps_rounded, 1)

            def step(s):
                for q in range(Q):
                    if has(s, 1):
                        k = s + 1
                        act.wait_ge(turned, k.at * Q + q + 1)
                        if k.res >= 2 and q == 0:
                            act.wait_ge(convolved, (k.at - 1) * GC)
                        nc.scalar.activation(
                            high[:, k.ring(2), q * QB:(q + 1) * QB, :, 1:CHUNKS + 1],
                            ps_turn[:, q % 2, :].rearrange("p (b c i) -> p b c i", b=QB, c=GC),
                            ACT.Identity).then_inc(high_ready, 1)
                    if has(s, 0):
                        act.wait_ge(convolved, s.at * GC + q + 1)
                        if s.res >= 2 and q == 0:
                            act.wait_ge(turned_back, (s.at - 1) * Q)
                        nc.scalar.activation(y[:, s.ring(2), :, q, :],
                                             ps_conv[:, q % 2, :].rearrange("p (b i) -> p b i", b=B),
                                             ACT.Identity).then_inc(y_ready, 1)
                    if q == 1 and finishes_norms(s):
                        lo, hi = norms(s)
                        act.wait_ge(var_ready, s.at + 3)
                        nc.scalar.activation(std[:, lo:hi, :],
                                             ps_var[:, lo * B:hi * B].rearrange("p (k b) -> p k b", b=B),
                                             ACT.Sqrt, bias=eps[:, 0:1]).then_inc(std_ready, 1)
                    if q == 0 and has(s, 1):
                        round_taps(s + 1)

            stage1(act, step)
            act.wait_ge(norm2_landed, 16)

            def unit(u):
                for half in range(2):
                    n = granule(u, half)
                    slot, buf = n.ring(GRING), n.ring(2)
                    act.wait_ge(x1_landed[slot], n.landings(GRING))
                    if n.res >= 2:
                        act.wait_ge(gn_split, n.at - 1)
                    src = tiles[:, slot, :].rearrange("p (i b e) -> p i b e", i=UCH, b=BH)
                    dst = gn[buf].rearrange("p (i b e) -> p i b e", i=UCH, b=BH)
                    for b in range(BH):
                        image = half * BH + b
                        last = nc.scalar.activation(dst[:, :, b, :], src[:, :, b, :], ACT.Identity,
                                                    scale=norm2[:, 0, image:image + 1],
                                                    bias=norm2[:, 1, image:image + 1])
                    last.then_inc(gn_ready, 1)
                    if half == 0:
                        act.wait_ge(rot_turned, u.at + 1)
                        if u.res >= 2:
                            act.wait_ge(rotated, (u.at - 1) * 2 * RH)
                        nc.scalar.activation(rot_hi[u.ring(2)], ps[:, 0, :], ACT.Identity).then_inc(rot_high, 1)

            stage2(act, unit)

        @block.vector
        def _(dve):
            nc.vector.memset(line[:], 0.0).then_inc(line_zeroed, 1)
            dve.wait_ge(line_zeroed, 1)
            dve.wait_ge(w_landed, 16)
            for places, sign in ((POS_IDX, 1.0), (NEG_IDX, -1.0)):
                for tap, place in enumerate(places):
                    dy, dx = place // KW - KH // 2, place % KW - KW // 2
                    at = (dy + 3) * PITCH + SLOT_MID + dx
                    nc.vector.tensor_scalar(line[:, at:at + 1], w_sb[:, tap + 1:tap + 2], sign, None,
                                            ALU.mult).then_inc(line_ready, 1)

            def step(s):
                now, later = s.ring(2), (s + 1).ring(2)
                for q in range(Q):
                    quarter = slice(q * QB, (q + 1) * QB)
                    if has(s, 1):
                        k = s + 1
                        dve.wait_ge(high_ready, k.at * Q + q + 1)
                        nc.vector.tensor_tensor(
                            low[:, k.ring(2), quarter, :, 1:CHUNKS + 1],
                            ps_turn[:, q % 2, :].rearrange("p (b c i) -> p b c i", b=QB, c=GC),
                            high[:, k.ring(2), quarter, :, 1:CHUNKS + 1].bitcast(F32),
                            ALU.subtract).then_inc(low_ready, 1)
                    if q == 2 and finishes_norms(s):
                        lo, hi = norms(s)
                        dve.wait_ge(std_ready, s.at + 3)
                        if has(s, 0):
                            dve.wait_ge(normed, s.at * Q + Q)
                        if has(s, -4):
                            dve.wait_ge(norm2_stored[now], (s + -4).landings(2))
                        nc.vector.reciprocal(affine[:, now, lo:hi, 0, :], std[:, lo:hi, :]
                                             ).then_inc(scale_ready, 1)
                    if has(s, -1):
                        k = s + -1
                        if q == 0 and k.res >= 2:
                            dve.wait_ge(x1_stored[k.ring(2)], k.landings(2) - 16)
                        dve.wait_ge(turned_back, k.at * Q + q + 1)
                        cols = slice(q * QB * P, (q + 1) * QB * P)
                        nc.vector.tensor_tensor(tiles[:, XRING + k.ring(2), cols], ps_back[:, q % 2, :],
                                                tiles[:, k.ring(XRING), cols], ALU.add).then_inc(x1_ready, 1)
                    if q == 0 and finishes_norms(s):
                        lo, hi = norms(s)
                        dve.wait_ge(mean_ready, s.at + 3)
                        cols = slice(lo * B, hi * B)
                        nc.vector.tensor_tensor(
                            dev[:, cols, :],
                            stats[:, now].rearrange("p k b f -> p (k b) f")[:, cols, 1:5:3],
                            ps_mean[:, cols].unsqueeze(2).broadcast_to([P, (hi - lo) * B, 2]),
                            ALU.subtract).then_inc(dev_ready, 1)
                    if q == 2 and finishes_norms(s):
                        lo, hi = norms(s)
                        dve.wait_ge(scale_ready, s.at + 3)
                        nc.vector.scalar_tensor_tensor(
                            out=affine[:, now, lo:hi, 1, :],
                            in0=ps_mean[:, lo * B:hi * B].rearrange("p (k b) -> p k b", b=B), scalar=-1.0,
                            in1=affine[:, now, lo:hi, 0, :], op0=ALU.mult, op1=ALU.mult
                        ).then_inc(affine_ready, 1)
                    if q == 0 and finishes_norms(s + -1):
                        dve.wait_ge(var_ready, s.at + 2)
                    if has(s, 3):
                        k = s + 3
                        if q == 0:
                            dve.wait_ge(x_landed[k.ring(2)], k.landings(2, 32))
                        for b in range(q * QB, (q + 1) * QB):
                            last = nc.vector.bn_stats(out=stats[:, later, 0, b, :],
                                                      in_=tiles[:, k.ring(XRING), b * P:(b + 1) * P])
                    if q == 0 and finishes_norms(s):
                        lo, hi = norms(s)
                        cols = slice(lo * B, hi * B)
                        dve.wait_ge(dev_ready, s.at + 3)
                        nc.vector.tensor_tensor(dev2[:, cols, :], dev[:, cols, :], dev[:, cols, :],
                                                ALU.mult).then_inc(dev2_ready, 1)
                    if has(s, -1):
                        k = s + -1
                        dve.wait_ge(x1_ready, k.at * Q + q + 1)
                        for b in range(q * QB, (q + 1) * QB):
                            last = nc.vector.bn_stats(out=stats[:, later, 1, b, :],
                                                      in_=tiles[:, XRING + k.ring(2), b * P:(b + 1) * P])
                if has(s, 3) or has(s, -1):
                    last.then_inc(stats_ready, 1)

            stage1(dve, step)

            def add_rows(u, half):
                n = granule(u, half)
                dst = tiles[:, n.ring(GRING), :].rearrange("p (i b r w) -> p i b r w", i=UCH, b=BH, r=ROWS)
                for h in range(RH):
                    dve.wait_ge(rotated, n.at * RH + h + 1)
                    xrow = dst[:, h // ROWS, :, h % ROWS, :]
                    nc.vector.tensor_tensor(
                        xrow, ps[:, n.ring(2) * RH + h, :].rearrange("p (b w) -> p b w", b=BH), xrow,
                        ALU.add).then_inc(out_ready, 1)

            def unit(u):
                for half in range(2):
                    n = granule(u, half)
                    dve.wait_ge(gn_ready, n.at + 1)
                    if n.res >= 2:
                        dve.wait_ge(rotated, (n.at - 1) * RH)
                    nc.vector.tensor_copy(gn_hi[n.ring(2)], gn[n.ring(2)]).then_inc(gn_high, 1)
                    if half == 1:
                        add_rows(u, 0)
                        continue
                    if u.res >= 1:
                        add_rows(u + -1, 1)
                    dve.wait_ge(rot_high, u.at + 1)
                    nc.vector.tensor_tensor(rot_lo[u.ring(2)], ps[:, 0, :], rot_hi[u.ring(2)].bitcast(F32),
                                            ALU.subtract).then_inc(rot_split, 1)

            stage2(dve, unit)
            add_rows(Step(UNITS - 1, UNITS - 1), 1)

        @block.tensor
        def _(pe):
            pe.wait_ge(consts_ready, 12)

            def products(dst, pairs):
                for n, (weights, moving) in enumerate(pairs):
                    last = nc.tensor.matmul(dst, weights, moving, start=(n == 0), stop=(n == len(pairs) - 1))
                return last

            def convolve(s, c):
                par = s.ring(2)
                if c == 0:
                    pe.wait_ge(low_ready, s.at * Q + Q)
                    pe.wait_ge(taps_split, s.at + 1)
                if s.res >= 1 or c >= 2:
                    pe.wait_ge(y_ready, s.at * GC + c - 1)
                pairs = []
                for j in (0, -1, 1):
                    slots = slice(2 * (1 - j), 2 * (1 - j) + 2)
                    hi_w = taps_hi[:, par, c, slots, :].rearrange("p s w -> p (s w)")
                    lo_w = taps_lo[:, par, c, slots, :].rearrange("p s w -> p (s w)")
                    hi_x = high[:, par, :, c, 1 + j:1 + j + CHUNKS]
                    lo_x = low[:, par, :, c, 1 + j:1 + j + CHUNKS]
                    pairs += [(hi_w, hi_x), (hi_w, lo_x), (lo_w, hi_x)]
                products(ps_conv[:, c % 2, :], pairs).then_inc(convolved, 1)

            def turn(k, q):
                pe.wait_ge(normed, k.at * Q + q + 1)
                if k.res >= 1 or q >= 2:
                    pe.wait_ge(low_ready, k.at * Q + q - 1)
                for n in range(QB):
                    last = nc.tensor.transpose(ps_turn[:, q % 2, n * P:(n + 1) * P], g[:, q * QB + n, :], ident[:])
                last.then_inc(turned, 1)

            def turn_back(k, q):
                if q == 0:
                    pe.wait_ge(y_ready, k.at * GC + GC)
                if k.res >= 1 or q >= 2:
                    pe.wait_ge(x1_ready, k.at * Q + q - 1)
                for n in range(QB):
                    last = nc.tensor.transpose(ps_back[:, q % 2, n * P:(n + 1) * P],
                                               y[:, k.ring(2), q * QB + n].rearrange("p c i -> p (c i)"), ident[:])
                last.then_inc(turned_back, 1)

            def step(s):
                for q in range(Q):
                    if has(s, 0):
                        convolve(s, q)
                    if finishes_norms(s) and q < 2:
                        lo, hi = norms(s)
                        cols = slice(lo * B, hi * B)
                        field = stats[:, s.ring(2)].rearrange("p k b f -> p (k b) f")
                        if q == 0:
                            pe.wait_ge(stats_ready, s.at + 3)
                            if finishes_norms(s + -1):
                                pe.wait_ge(affine_ready, s.at + 2)
                            products(ps_mean[:, cols], [(ones_half[:], field[:, cols, 1]),
                                                        (ones_half[:], field[:, cols, 4])]).then_inc(mean_ready, 1)
                        else:
                            pe.wait_ge(dev2_ready, s.at + 3)
                            products(ps_var[:, cols], [(ones_half[:], dev2[:, cols, 0]),
                                                       (ones_half[:], dev2[:, cols, 1]),
                                                       (ones_all[:], field[:, cols, 2]),
                                                       (ones_all[:], field[:, cols, 5])]).then_inc(var_ready, 1)
                    if has(s, 1):
                        turn(s + 1, q)
                    if has(s, -1):
                        turn_back(s + -1, q)

            stage1(pe, step)

            def turn_rotations(u):
                par = u.ring(2)
                pe.wait_ge(rot_landed[par], u.landings(2))
                if u.res >= 1:
                    pe.wait_ge(out_ready, (u.at - 1) * 2 * RH + 1)
                    pe.wait_ge(rot_split, u.at)
                for h in range(RH):
                    last = nc.tensor.transpose(ps[:, 0, h * P:(h + 1) * P], rot_raw[par][:, h * C:(h + 1) * C],
                                               ident[:])
                last.then_inc(rot_turned, 1)

            turn_rotations(Step(0, 0))

            def unit(u):
                pe.wait_ge(rot_split, u.at + 1)
                par = u.ring(2)
                for half in range(2):
                    n = granule(u, half)
                    buf = n.ring(2)
                    pe.wait_ge(gn_split, n.at + 1)
                    hi_x = gn_hi[buf].rearrange("p (i b r w) -> p i b r w", i=UCH, b=BH, r=ROWS)
                    lo_x = gn_lo[buf].rearrange("p (i b r w) -> p i b r w", i=UCH, b=BH, r=ROWS)
                    for h in range(RH):
                        if n.res >= 2:
                            pe.wait_ge(out_ready, (n.at - 2) * RH + h + 1)
                        hi_w, lo_w = (t[par][:, h * P:(h + 1) * P] for t in (rot_hi, rot_lo))
                        at = (h // ROWS, slice(None), h % ROWS)
                        products(ps[:, n.ring(2) * RH + h, :],
                                 [(hi_w, hi_x[:, at[0], :, at[2], :]), (hi_w, lo_x[:, at[0], :, at[2], :]),
                                  (lo_w, hi_x[:, at[0], :, at[2], :])]).then_inc(rotated, 1)
                    if half == 0 and u.res + 1 < UNITS:
                        turn_rotations(u + 1)

            stage2(pe, unit)


_INS = ['x', 'L0_conv_weight', 'L1_conv_rota_matrix']
_OUTS = [((B, C, H, W), 'float32')]


def kernel(**inputs):
    import numpy as _np
    import concourse.bacc as _bacc
    from concourse import mybir as _mybir
    from concourse.bass_utils import run_bass_kernel_spmd as _run

    nc = _bacc.Bacc("TRN2", target_bir_lowering=False, num_devices=1)
    arrays, args = {}, []
    for name in _INS:
        a = _np.ascontiguousarray(inputs[name])
        arrays[f"in_{name}_dram"] = a
        args.append(nc.dram_tensor(f"in_{name}_dram", a.shape, _mybir.dt.from_np(a.dtype), kind="ExternalInput").ap())
    for i, (shape, dtype) in enumerate(_OUTS):
        dt = _mybir.dt.from_np(_np.dtype(dtype))
        args.append(nc.dram_tensor(f"out_{i}_dram", shape, dt, kind="ExternalOutput").ap())
    conv_rotate_kernel(nc, *args)
    r = _run(nc, [arrays], core_ids=[0])
    got = tuple(r.results[0][f"out_{i}_dram"] for i in range(len(_OUTS)))
    return got[0]
```

```python
from contextlib import ExitStack

import concourse.bass as bass
from concourse import mybir

F32 = mybir.dt.float32
F32R = mybir.dt.float32r
ALU = mybir.AluOpType
ACT = mybir.ActivationFunctionType

P = 128
B, C, H, W = 16, 128, 64, 64
GC = 4
GROUPS = C // GC
ROWS = P // W
CHUNKS = H // ROWS
Q = 4
QB = B // Q
EPS = 1e-5

PITCH = W + 2
SLOT_MID = W - 1
WINDOW = 6 * PITCH
LINE = 528
KH = KW = 5
POS_IDX = (0, 2, 4, 10, 14, 20, 22, 24)
NEG_IDX = (6, 7, 8, 11, 13, 16, 17, 18)

XRING = 8
XAHEAD = 5
UNROLL = 8
FIRST_STEP, LAST_STEP = -4, GROUPS + 1
LOOP_START, LOOP_TRIPS = 3, 3

UCH = 2
RH = UCH * ROWS
BH = B // 2
UNITS = CHUNKS // UCH
GCOLS = UCH * BH * P
GRING = 8
AHEAD = 6
UUNROLL = GRING // 2
ULOOP_START, ULOOP_TRIPS = UUNROLL, UNITS // UUNROLL - 2


class Step:

    def __init__(self, at, res):
        self.at, self.res = at, res

    def __add__(self, n):
        return Step(self.at + n, self.res + n)

    def ring(self, n):
        return self.res % n

    def landings(self, n, each=16):
        return (self.at - self.ring(n)) * (each // n) + each

    def of(self, ap):
        if isinstance(self.at, int):
            return ap[self.at]
        part = ap[bass.ds(self.at, 1)]
        names = " ".join("abcdefg"[:len(part.shape) - 2])
        return part.rearrange(f"o p {names} -> (o p) {names}")


def conv_rotate_kernel(nc, x, weight, rota, out):
    tap_lines = nc.dram_tensor("tap_lines", (C, LINE), F32, kind="Internal").ap()
    x1_dram = nc.dram_tensor("x1_scratch", (C, CHUNKS, B, P), F32, kind="Internal").ap()
    norm2_dram = nc.dram_tensor("norm2_scratch", (C, 2 * B), F32, kind="Internal").ap()

    x_src = x.rearrange("b (g c) (i r) w -> g (c i) b (r w)", c=GC, r=ROWS)
    x1_dst = x1_dram.rearrange("(g c) i b e -> g (c i) (b e)", c=GC)
    norm2_dst = norm2_dram.rearrange("(g c) k -> g c k", c=GC)
    x1_src = [x1_dram[:, :, n * BH:(n + 1) * BH, :].rearrange("c (u i) b e -> u c i (b e)", i=UCH) for n in range(2)]
    out_dst = [[out[n * BH:(n + 1) * BH].rearrange("b c (u i r) w -> u i c b (r w)", i=UCH, r=ROWS)[:, i]
                for i in range(UCH)] for n in range(2)]
    rota_src = rota.rearrange("(u h) v c -> u v h c", h=RH)

    with ExitStack() as ctx:
        def sb(name, shape, dt=F32):
            return ctx.enter_context(nc.sbuf_tensor(name, shape, dt))

        def sem(name):
            return ctx.enter_context(nc.semaphore(name))

        tiles = sb("tiles", [P, XRING + 2, B * P])
        g = sb("g", [P, B, P])
        high = sb("high", [P, 2, B, GC, CHUNKS + 2], F32R)
        low = sb("low", [P, 2, B, GC, CHUNKS + 2], F32R)
        y = sb("y", [P, 2, B, GC, CHUNKS])
        taps_raw = sb("taps_raw", [P, 2, GC, 6, PITCH])
        taps_hi = sb("taps_hi", [P, 2, GC, 6, W], F32R)
        taps_lo = sb("taps_lo", [P, 2, GC, 6, W], F32R)
        line = sb("line", [C, LINE])
        w_sb = sb("w_sb", [C, 9])
        ident = sb("ident", [P, P])
        ones_mean = sb("ones_mean", [P, P])
        ones_var = sb("ones_var", [P, P])
        eps = sb("eps", [P, 1])
        carrier = sb("carrier", [P, Q])
        stats = sb("stats", [P, 2, 2, B, 3])
        dev = sb("dev", [P, 2 * B])
        dev2 = sb("dev2", [P, 2 * B])
        std = sb("std", [P, 2, B])
        affine = sb("affine", [P, 2, 2, 2, B])
        norm2 = sb("norm2", [C, 2, B])

        ps = ctx.enter_context(nc.psum_tensor("ps", [P, 8, 512], F32))
        ps_turn = ps[:, 0:2, :]
        ps_conv = ps[:, 2:4, :]
        ps_back = ps[:, 4:6, :]
        ps_mean = ps[:, 6, 0:2 * B]
        ps_var = ps[:, 7, 0:2 * B]

        def flat(t, n, cols):
            return t[:, n].rearrange("p a b c -> p (a b c)")[:, 0:cols]

        gn = [flat(y, n, GCOLS) for n in range(2)]
        gn_hi = [flat(high, n, GCOLS) for n in range(2)]
        gn_lo = [flat(low, n, GCOLS) for n in range(2)]
        rot_raw = [flat(taps_raw, n, RH * C) for n in range(2)]
        rot_hi = [flat(taps_hi, n, RH * C) for n in range(2)]
        rot_lo = [flat(taps_lo, n, RH * C) for n in range(2)]

        w_landed = sem("w_landed")
        line_zeroed = sem("line_zeroed")
        line_ready = sem("line_ready")
        line_stored = sem("line_stored")
        ident_zeroed = sem("ident_zeroed")
        consts_ready = sem("consts_ready")
        x_landed = [sem(f"x_landed{n}") for n in range(2)]
        taps_landed = [sem(f"taps_landed{n}") for n in range(2)]
        taps_rounded = sem("taps_rounded")
        taps_split = sem("taps_split")
        stats_ready = sem("stats_ready")
        mean_ready = sem("mean_ready")
        dev_ready = sem("dev_ready")
        dev2_ready = sem("dev2_ready")
        var_ready = sem("var_ready")
        std_ready = sem("std_ready")
        scale_ready = sem("scale_ready")
        affine_ready = sem("affine_ready")
        normed = sem("normed")
        turned = sem("turned")
        high_ready = sem("high_ready")
        low_ready = sem("low_ready")
        convolved = sem("convolved")
        y_ready = sem("y_ready")
        turned_back = sem("turned_back")
        x1_ready = sem("x1_ready")
        x1_stored = [sem(f"x1_stored{n}") for n in range(2)]
        norm2_stored = [sem(f"norm2_stored{n}") for n in range(2)]
        norm2_landed = sem("norm2_landed")
        x1_landed = [sem(f"x1_landed{n}") for n in range(GRING)]
        rot_landed = [sem(f"rot_landed{n}") for n in range(2)]
        rot_turned = sem("rot_turned")
        rot_high = sem("rot_high")
        rot_split = sem("rot_split")
        gn_ready = sem("gn_ready")
        gn_high = sem("gn_high")
        gn_split = sem("gn_split")
        rotated = sem("rotated")
        out_ready = sem("out_ready")
        out_stored = [sem(f"out_stored{n}") for n in range(GRING)]

        block = ctx.enter_context(nc.Block())

        def has(s, shift):
            return 0 <= s.res + shift < GROUPS

        def norms(s):
            return 0 if has(s, 3) else 1, 2 if has(s, -2) else 1

        def finishes_norms(s):
            return has(s, 3) or has(s, -2)

        def turns(s, q):
            k, quarter = (s + 1, q + 1) if q + 1 < Q else (s + 2, 0)
            return (k, quarter) if has(k, 0) else None

        def normalises(s, q):
            k, quarter = (s + 1, q + 3) if q + 3 < Q else (s + 2, q + 3 - Q)
            return (k, quarter) if has(k, 0) else None

        def stage1(engine, step):
            for s in range(FIRST_STEP, LOOP_START):
                step(Step(s, s))
            with engine.Fori(0, LOOP_TRIPS) as trip:
                for t in range(UNROLL):
                    step(Step(trip * UNROLL + (LOOP_START + t), LOOP_START + t))
            for s in range(LOOP_START + LOOP_TRIPS * UNROLL, LAST_STEP + 1):
                step(Step(s, s))

        def stage2(engine, unit):
            for u in range(ULOOP_START):
                unit(Step(u, u))
            with engine.Fori(0, ULOOP_TRIPS) as trip:
                for t in range(UUNROLL):
                    unit(Step(trip * UUNROLL + (ULOOP_START + t), ULOOP_START + t))
            for u in range(UNITS - UUNROLL, UNITS):
                unit(Step(u, u))

        def granule(u, half):
            return Step(u.at * 2 + half, u.res * 2 + half)

        @block.sync
        def _(sp):
            sp.dma_start(w_sb[:], weight.rearrange("c o a b -> c (o a b)")).then_inc(w_landed, 16)

            def load(k):
                par = k.ring(2)
                if k.res >= 2:
                    sp.wait_ge(x_landed[par], k.landings(2, 32) - 32)
                x_slot = tiles[:, k.ring(XRING), :].rearrange("p (b e) -> p b e", b=B)
                for half in (slice(0, BH), slice(BH, B)):
                    sp.dma_start(x_slot[:, half], k.of(x_src)[:, half]).then_inc(x_landed[par], 16)

            def load_taps(k):
                par = k.ring(2)
                if k.res >= 2:
                    sp.wait_ge(taps_split, k.at - 1)
                for r in range(ROWS):
                    window = bass.AP(tensor=tap_lines.tensor, offset=k.at * (GC * LINE) + r * PITCH,
                                     ap=[[1, W], [LINE, GC], [1, WINDOW]])
                    sp.dma_start(taps_raw[r * W:(r + 1) * W, par].rearrange("p c s w -> p c (s w)"),
                                 window).then_inc(taps_landed[par], 16)

            for k in range(2):
                load(Step(k, k))
            sp.wait_ge(line_ready, len(POS_IDX + NEG_IDX))
            sp.dma_start(tap_lines, line[:]).then_inc(line_stored, 16)
            sp.wait_ge(line_stored, 16)
            for k in range(2):
                load_taps(Step(k, k))
            for k in range(2, XRING):
                load(Step(k, k))

            def step(s):
                if s.res >= 0 and has(s, 2):
                    load_taps(s + 2)
                if s.res >= XRING - XAHEAD and has(s, XAHEAD):
                    k = s + XAHEAD
                    sp.wait_ge(x1_ready, (k.at - XRING + 1) * Q)
                    load(k)
                if has(s, -2):
                    k = s + -2
                    sp.wait_ge(affine_ready, s.at + 4)
                    sp.dma_start(k.of(norm2_dst), affine[0:GC, s.ring(2), 1].rearrange("p a b -> p (a b)")
                                 ).then_inc(norm2_stored[k.ring(2)], 16)
                if has(s, -1):
                    k = s + -1
                    sp.wait_ge(x1_ready, k.at * Q + Q)
                    sp.dma_start(k.of(x1_dst), tiles[:, XRING + k.ring(2), :]
                                 ).then_inc(x1_stored[k.ring(2)], 16)

            stage1(sp, step)

            for n in range(2):
                sp.wait_ge(x1_stored[n], 16 * (GROUPS // 2))
                sp.wait_ge(norm2_stored[n], 16 * (GROUPS // 2))
            sp.dma_start(norm2[:], norm2_dram.rearrange("c (a b) -> c a b", a=2)).then_inc(norm2_landed, 16)

            def load_granule(u, half):
                n = granule(u, half)
                slot = n.ring(GRING)
                if n.res >= GRING:
                    sp.wait_ge(out_stored[slot], n.landings(GRING, 16 * UCH) - 16 * UCH)
                sp.dma_start(tiles[:, slot, :].rearrange("p (i f) -> p i f", i=UCH), u.of(x1_src[half])
                             ).then_inc(x1_landed[slot], 16)

            def load_rotations(u):
                if u.res >= 2:
                    sp.wait_ge(rot_turned, u.at - 1)
                sp.dma_start(rot_raw[u.ring(2)].rearrange("v (h c) -> v h c", h=RH), u.of(rota_src)
                             ).then_inc(rot_landed[u.ring(2)], 16)

            def store_granule(u, half):
                n = granule(u, half)
                slot = n.ring(GRING)
                sp.wait_ge(out_ready, n.at * RH + RH)
                for i in range(UCH):
                    sp.dma_start(u.of(out_dst[half][i]),
                                 tiles[:, slot, :].rearrange("p (i b e) -> p i b e", i=UCH, b=BH)[:, i]
                                 ).then_inc(out_stored[slot], 16)

            for u in range(AHEAD // 2):
                if u < 2:
                    load_rotations(Step(u, u))
                for half in range(2):
                    load_granule(Step(u, u), half)

            def unit(u):
                if u.res + 2 < UNITS:
                    load_rotations(u + 2)
                for half in range(2):
                    store_granule(u, half)
                    if u.res + AHEAD // 2 < UNITS:
                        load_granule(u + AHEAD // 2, half)

            stage2(sp, unit)
            for slot in range(GRING):
                sp.wait_ge(out_stored[slot], 16 * UCH * (2 * UNITS // GRING))

        @block.gpsimd
        def _(pool):
            nc.gpsimd.memset(ident[:], 0.0).then_inc(ident_zeroed, 1)
            nc.gpsimd.memset(ones_mean[:], 1.0 / P).then_inc(consts_ready, 1)
            nc.gpsimd.memset(ones_var[:], 1.0 / (P * P)).then_inc(consts_ready, 1)
            nc.gpsimd.memset(eps[:], EPS).then_inc(consts_ready, 1)
            pool.wait_ge(ident_zeroed, 1)
            nc.gpsimd.affine_select(out=ident[:], in_=ident[:], compare_op=ALU.not_equal, fill=1.0, base=0,
                                    pattern=[[-1, P]], channel_multiplier=1).then_inc(consts_ready, 1)
            for t in (high, low):
                for n in range(2):
                    for end in (0, CHUNKS + 1):
                        nc.gpsimd.memset(t[:, n, :, :, end:end + 1].bitcast(F32), 0.0).then_inc(consts_ready, 1)

            pool.wait_ge(consts_ready, 4)

            def normalise(k, q):
                pool.wait_ge(affine_ready, k.at + 1)
                if k.res >= 1:
                    pool.wait_ge(turned, (k.at - 1) * Q + q + 1)
                nc.gpsimd.tensor_tensor(carrier[:, q:q + 1], eps[:], eps[:], ALU.mult)
                for b in range(q * QB, (q + 1) * QB):
                    last = nc.gpsimd.tensor_scalar(g[:, b, :], tiles[:, k.ring(XRING), b * P:(b + 1) * P],
                                                   affine[:, (k + 1).ring(2), 0, 0, b:b + 1],
                                                   affine[:, (k + 1).ring(2), 0, 1, b:b + 1], ALU.mult, ALU.add)
                last.then_inc(normed, 1)

            def split_taps(k):
                par = k.ring(2)
                pool.wait_ge(taps_rounded, k.at + 1)
                nc.gpsimd.tensor_tensor(taps_lo[:, par], taps_raw[:, par, :, ::-1, W - 1::-1],
                                        taps_hi[:, par].bitcast(F32), ALU.subtract).then_inc(taps_split, 1)

            def step(s):
                for q in range(Q):
                    if normalises(s, q):
                        normalise(*normalises(s, q))
                    if q == 1 and has(s, 1):
                        split_taps(s + 1)

            stage1(pool, step)

            def unit(u):
                for half in range(2):
                    n = granule(u, half)
                    buf = n.ring(2)
                    pool.wait_ge(gn_high, n.at + 1)
                    if n.res >= 2:
                        pool.wait_ge(rotated, (n.at - 1) * RH)
                    nc.gpsimd.tensor_tensor(gn_lo[buf], gn[buf], gn_hi[buf].bitcast(F32),
                                            ALU.subtract).then_inc(gn_split, 1)

            stage2(pool, unit)

        @block.scalar
        def _(act):
            act.wait_ge(consts_ready, 4)

            def round_taps(k):
                par = k.ring(2)
                act.wait_ge(taps_landed[par], k.landings(2, 16 * ROWS))
                if k.res >= 2:
                    act.wait_ge(convolved, (k.at - 1) * GC)
                nc.scalar.activation(taps_hi[:, par], taps_raw[:, par, :, ::-1, W - 1::-1],
                                     ACT.Identity).then_inc(taps_rounded, 1)

            def step(s):
                for q in range(Q):
                    if has(s, 0):
                        act.wait_ge(convolved, s.at * GC + q + 1)
                        if s.res >= 2 and q == 0:
                            act.wait_ge(turned_back, (s.at - 1) * Q)
                        nc.scalar.activation(y[:, s.ring(2), :, q, :],
                                             ps_conv[:, q % 2, :].rearrange("p (b i) -> p b i", b=B),
                                             ACT.Identity).then_inc(y_ready, 1)
                    if turns(s, q):
                        k, t = turns(s, q)
                        act.wait_ge(turned, k.at * Q + t + 1)
                        if k.res >= 2 and t == 0:
                            act.wait_ge(convolved, (k.at - 1) * GC)
                        nc.scalar.activation(
                            high[:, k.ring(2), t * QB:(t + 1) * QB, :, 1:CHUNKS + 1],
                            ps_turn[:, t % 2, :].rearrange("p (b c i) -> p b c i", b=QB, c=GC),
                            ACT.Identity).then_inc(high_ready, 1)
                    if q == 3 and finishes_norms(s):
                        lo, hi = norms(s)
                        act.wait_ge(var_ready, s.at + 4)
                        nc.scalar.activation(std[:, lo:hi, :],
                                             ps_var[:, lo * B:hi * B].rearrange("p (k b) -> p k b", b=B),
                                             ACT.Sqrt, bias=eps[:, 0:1]).then_inc(std_ready, 1)
                    if q == 0 and has(s, 1):
                        round_taps(s + 1)

            stage1(act, step)
            act.wait_ge(norm2_landed, 16)

            def unit(u):
                for half in range(2):
                    n = granule(u, half)
                    slot, buf = n.ring(GRING), n.ring(2)
                    act.wait_ge(x1_landed[slot], n.landings(GRING))
                    if n.res >= 2:
                        act.wait_ge(gn_split, n.at - 1)
                    src = tiles[:, slot, :].rearrange("p (i b e) -> p i b e", i=UCH, b=BH)
                    dst = gn[buf].rearrange("p (i b e) -> p i b e", i=UCH, b=BH)
                    for b in range(BH):
                        image = half * BH + b
                        last = nc.scalar.activation(dst[:, :, b, :], src[:, :, b, :], ACT.Identity,
                                                    scale=norm2[:, 0, image:image + 1],
                                                    bias=norm2[:, 1, image:image + 1])
                    last.then_inc(gn_ready, 1)
                    if half == 0:
                        act.wait_ge(rot_turned, u.at + 1)
                        if u.res >= 2:
                            act.wait_ge(rotated, (u.at - 1) * 2 * RH)
                        nc.scalar.activation(rot_hi[u.ring(2)], ps[:, 0, :], ACT.Identity).then_inc(rot_high, 1)

            stage2(act, unit)

        @block.vector
        def _(dve):
            nc.vector.memset(line[:], 0.0).then_inc(line_zeroed, 1)
            dve.wait_ge(line_zeroed, 1)
            dve.wait_ge(w_landed, 16)
            for places, sign in ((POS_IDX, 1.0), (NEG_IDX, -1.0)):
                for tap, place in enumerate(places):
                    dy, dx = place // KW - KH // 2, place % KW - KW // 2
                    at = (dy + 3) * PITCH + SLOT_MID + dx
                    nc.vector.tensor_scalar(line[:, at:at + 1], w_sb[:, tap + 1:tap + 2], sign, None,
                                            ALU.mult).then_inc(line_ready, 1)

            def step(s):
                now, later = s.ring(2), (s + 1).ring(2)
                lo, hi = norms(s)
                cols = slice(lo * B, hi * B)

                def statistics(norm, tile, q):
                    for b in range(q * QB, (q + 1) * QB, 2):
                        last = nc.vector.bn_stats(out=stats[:, later, norm, b:b + 2, :].rearrange("p b f -> p (b f)"),
                                                  in_=tile[:, b * P:(b + 2) * P].rearrange("p (b e) -> p e b", b=2))
                    return last

                for q in range(Q):
                    if turns(s, q):
                        k, t = turns(s, q)
                        quarter = slice(t * QB, (t + 1) * QB)
                        dve.wait_ge(high_ready, k.at * Q + t + 1)
                        nc.vector.tensor_tensor(
                            low[:, k.ring(2), quarter, :, 1:CHUNKS + 1],
                            ps_turn[:, t % 2, :].rearrange("p (b c i) -> p b c i", b=QB, c=GC),
                            high[:, k.ring(2), quarter, :, 1:CHUNKS + 1].bitcast(F32),
                            ALU.subtract).then_inc(low_ready, 1)
                    if q == 2 and finishes_norms(s):
                        dve.wait_ge(mean_ready, s.at + 4)
                        nc.vector.tensor_tensor(
                            dev[:, cols], stats[:, now].rearrange("p k b f -> p (k b) f")[:, cols, 1],
                            ps_mean[:, cols], ALU.subtract).then_inc(dev_ready, 1)
                    if has(s, -1):
                        k = s + -1
                        if q == 0 and k.res >= 2:
                            dve.wait_ge(x1_stored[k.ring(2)], k.landings(2) - 16)
                        dve.wait_ge(turned_back, k.at * Q + q + 1)
                        quarter = slice(q * QB * P, (q + 1) * QB * P)
                        nc.vector.tensor_tensor(tiles[:, XRING + k.ring(2), quarter], ps_back[:, q % 2, :],
                                                tiles[:, k.ring(XRING), quarter], ALU.add).then_inc(x1_ready, 1)
                    if q == 2 and finishes_norms(s):
                        dve.wait_ge(dev_ready, s.at + 4)
                        nc.vector.tensor_tensor(dev2[:, cols], dev[:, cols], dev[:, cols], ALU.mult).then_inc(dev2_ready, 1)
                    if q == 0 and finishes_norms(s + -1):
                        dve.wait_ge(var_ready, s.at + 3)
                    if has(s, 4):
                        k = s + 4
                        if q == 0:
                            dve.wait_ge(x_landed[k.ring(2)], k.landings(2, 32))
                        last = statistics(0, tiles[:, k.ring(XRING)], q)
                    if has(s, -1):
                        k = s + -1
                        dve.wait_ge(x1_ready, k.at * Q + q + 1)
                        last = statistics(1, tiles[:, XRING + k.ring(2)], q)
                if has(s, 4) or has(s, -1):
                    last.then_inc(stats_ready, 1)
                if finishes_norms(s):
                    dve.wait_ge(std_ready, s.at + 4)
                    if has(s, 1):
                        dve.wait_ge(normed, s.at * Q + 2 * Q)
                    if has(s, -3):
                        dve.wait_ge(norm2_stored[later], (s + -3).landings(2))
                    nc.vector.reciprocal(affine[:, now, lo:hi, 0, :], std[:, lo:hi, :]).then_inc(scale_ready, 1)
                    dve.wait_ge(scale_ready, s.at + 4)
                    nc.vector.scalar_tensor_tensor(
                        out=affine[:, now, lo:hi, 1, :],
                        in0=ps_mean[:, cols].rearrange("p (k b) -> p k b", b=B), scalar=-1.0,
                        in1=affine[:, now, lo:hi, 0, :], op0=ALU.mult, op1=ALU.mult).then_inc(affine_ready, 1)

            stage1(dve, step)

            def add_rows(u, half):
                n = granule(u, half)
                dst = tiles[:, n.ring(GRING), :].rearrange("p (i b r w) -> p i b r w", i=UCH, b=BH, r=ROWS)
                for h in range(RH):
                    dve.wait_ge(rotated, n.at * RH + h + 1)
                    xrow = dst[:, h // ROWS, :, h % ROWS, :]
                    nc.vector.tensor_tensor(
                        xrow, ps[:, n.ring(2) * RH + h, :].rearrange("p (b w) -> p b w", b=BH), xrow,
                        ALU.add).then_inc(out_ready, 1)

            def unit(u):
                for half in range(2):
                    n = granule(u, half)
                    dve.wait_ge(gn_ready, n.at + 1)
                    if n.res >= 2:
                        dve.wait_ge(rotated, (n.at - 1) * RH)
                    nc.vector.tensor_copy(gn_hi[n.ring(2)], gn[n.ring(2)]).then_inc(gn_high, 1)
                    if half == 1:
                        add_rows(u, 0)
                        continue
                    if u.res >= 1:
                        add_rows(u + -1, 1)
                    dve.wait_ge(rot_high, u.at + 1)
                    nc.vector.tensor_tensor(rot_lo[u.ring(2)], ps[:, 0, :], rot_hi[u.ring(2)].bitcast(F32),
                                            ALU.subtract).then_inc(rot_split, 1)

            stage2(dve, unit)
            add_rows(Step(UNITS - 1, UNITS - 1), 1)

        @block.tensor
        def _(pe):
            pe.wait_ge(consts_ready, 12)

            def products(dst, pairs):
                for n, (weights, moving) in enumerate(pairs):
                    last = nc.tensor.matmul(dst, weights, moving, start=(n == 0), stop=(n == len(pairs) - 1))
                return last

            def convolve(s, c):
                par = s.ring(2)
                if c == 0:
                    pe.wait_ge(low_ready, s.at * Q + Q)
                    pe.wait_ge(taps_split, s.at + 1)
                if s.res >= 1 or c >= 2:
                    pe.wait_ge(y_ready, s.at * GC + c - 1)
                pairs = []
                for j in (0, -1, 1):
                    slots = slice(2 * (1 - j), 2 * (1 - j) + 2)
                    hi_w = taps_hi[:, par, c, slots, :].rearrange("p s w -> p (s w)")
                    lo_w = taps_lo[:, par, c, slots, :].rearrange("p s w -> p (s w)")
                    hi_x = high[:, par, :, c, 1 + j:1 + j + CHUNKS]
                    lo_x = low[:, par, :, c, 1 + j:1 + j + CHUNKS]
                    pairs += [(hi_w, hi_x), (hi_w, lo_x), (lo_w, hi_x)]
                products(ps_conv[:, c % 2, :], pairs).then_inc(convolved, 1)

            def turn(k, q):
                pe.wait_ge(normed, k.at * Q + q + 1)
                if k.res >= 1 or q >= 2:
                    pe.wait_ge(low_ready, k.at * Q + q - 1)
                for n in range(QB):
                    last = nc.tensor.transpose(ps_turn[:, q % 2, n * P:(n + 1) * P], g[:, q * QB + n, :], ident[:])
                last.then_inc(turned, 1)

            def turn_back(k, q):
                if q == 0:
                    pe.wait_ge(y_ready, k.at * GC + GC)
                if k.res >= 1 or q >= 2:
                    pe.wait_ge(x1_ready, k.at * Q + q - 1)
                for n in range(QB):
                    last = nc.tensor.transpose(ps_back[:, q % 2, n * P:(n + 1) * P],
                                               y[:, k.ring(2), q * QB + n].rearrange("p c i -> p (c i)"), ident[:])
                last.then_inc(turned_back, 1)

            def step(s):
                for q in range(Q):
                    if has(s, 0):
                        convolve(s, q)
                    if finishes_norms(s) and q in (1, 3):
                        lo, hi = norms(s)
                        cols = slice(lo * B, hi * B)
                        field = stats[:, s.ring(2)].rearrange("p k b f -> p (k b) f")
                        if q == 1:
                            pe.wait_ge(stats_ready, s.at + 4)
                            if finishes_norms(s + -1):
                                pe.wait_ge(affine_ready, s.at + 3)
                            products(ps_mean[:, cols], [(ones_mean[:], field[:, cols, 1])]).then_inc(mean_ready, 1)
                        else:
                            pe.wait_ge(dev2_ready, s.at + 4)
                            products(ps_var[:, cols], [(ones_var[:], field[:, cols, 2]),
                                                       (ones_mean[:], dev2[:, cols])]).then_inc(var_ready, 1)
                    if turns(s, q):
                        turn(*turns(s, q))
                    if has(s, -1):
                        turn_back(s + -1, q)

            stage1(pe, step)

            def turn_rotations(u):
                par = u.ring(2)
                pe.wait_ge(rot_landed[par], u.landings(2))
                if u.res >= 1:
                    pe.wait_ge(out_ready, (u.at - 1) * 2 * RH + 1)
                    pe.wait_ge(rot_split, u.at)
                for h in range(RH):
                    last = nc.tensor.transpose(ps[:, 0, h * P:(h + 1) * P], rot_raw[par][:, h * C:(h + 1) * C],
                                               ident[:])
                last.then_inc(rot_turned, 1)

            turn_rotations(Step(0, 0))

            def unit(u):
                pe.wait_ge(rot_split, u.at + 1)
                par = u.ring(2)
                for half in range(2):
                    n = granule(u, half)
                    buf = n.ring(2)
                    pe.wait_ge(gn_split, n.at + 1)
                    hi_x = gn_hi[buf].rearrange("p (i b r w) -> p i b r w", i=UCH, b=BH, r=ROWS)
                    lo_x = gn_lo[buf].rearrange("p (i b r w) -> p i b r w", i=UCH, b=BH, r=ROWS)
                    for h in range(RH):
                        if n.res >= 2:
                            pe.wait_ge(out_ready, (n.at - 2) * RH + h + 1)
                        hi_w, lo_w = (t[par][:, h * P:(h + 1) * P] for t in (rot_hi, rot_lo))
                        at = (h // ROWS, slice(None), h % ROWS)
                        products(ps[:, n.ring(2) * RH + h, :],
                                 [(hi_w, hi_x[:, at[0], :, at[2], :]), (hi_w, lo_x[:, at[0], :, at[2], :]),
                                  (lo_w, hi_x[:, at[0], :, at[2], :])]).then_inc(rotated, 1)
                    if half == 0 and u.res + 1 < UNITS:
                        turn_rotations(u + 1)

            stage2(pe, unit)


_INS = ['x', 'L0_conv_weight', 'L1_conv_rota_matrix']
_OUTS = [((B, C, H, W), 'float32')]


def kernel(**inputs):
    import numpy as _np
    import concourse.bacc as _bacc
    from concourse import mybir as _mybir
    from concourse.bass_utils import run_bass_kernel_spmd as _run

    nc = _bacc.Bacc("TRN2", target_bir_lowering=False, num_devices=1)
    arrays, args = {}, []
    for name in _INS:
        a = _np.ascontiguousarray(inputs[name])
        arrays[f"in_{name}_dram"] = a
        args.append(nc.dram_tensor(f"in_{name}_dram", a.shape, _mybir.dt.from_np(a.dtype), kind="ExternalInput").ap())
    for i, (shape, dtype) in enumerate(_OUTS):
        dt = _mybir.dt.from_np(_np.dtype(dtype))
        args.append(nc.dram_tensor(f"out_{i}_dram", shape, dt, kind="ExternalOutput").ap())
    conv_rotate_kernel(nc, *args)
    r = _run(nc, [arrays], core_ids=[0])
    got = tuple(r.results[0][f"out_{i}_dram"] for i in range(len(_OUTS)))
    return got[0]
```

```python
from contextlib import ExitStack

import concourse.bass as bass
from concourse import mybir

F32 = mybir.dt.float32
F32R = mybir.dt.float32r
ALU = mybir.AluOpType
ACT = mybir.ActivationFunctionType

P = 128
B, C, H, W = 16, 128, 64, 64
GC = 4
GROUPS = C // GC
ROWS = P // W
CHUNKS = H // ROWS
Q = 4
QB = B // Q
POOL_QB = QB - 1
EPS = 1e-5

PITCH = W + 2
SLOT_MID = W - 1
WINDOW = 6 * PITCH
LINE = 528
KH = KW = 5
POS_IDX = (0, 2, 4, 10, 14, 20, 22, 24)
NEG_IDX = (6, 7, 8, 11, 13, 16, 17, 18)

XRING = 8
XAHEAD = 5
UNROLL = 8
FIRST_STEP, LAST_STEP = -4, GROUPS + 1
LOOP_START, LOOP_TRIPS = 3, 3

ROT_LOADS = 4

UCH = 2
RH = UCH * ROWS
BH = B // 2
UNITS = CHUNKS // UCH
GCOLS = UCH * BH * P
GRING = 8
AHEAD = 6
EARLY_STEPS = (GROUPS - 2, GROUPS - 1, GROUPS - 1, GROUPS)
UUNROLL = GRING // 2
ULOOP_START, ULOOP_TRIPS = UUNROLL, UNITS // UUNROLL - 2


class Step:

    def __init__(self, at, res):
        self.at, self.res = at, res

    def __add__(self, n):
        return Step(self.at + n, self.res + n)

    def ring(self, n):
        return self.res % n

    def landings(self, n, each=16):
        return (self.at - self.ring(n)) * (each // n) + each

    def rows(self, n):
        return slice(self.at * n, self.at * n + n) if isinstance(self.at, int) else bass.ds(self.at * n, n)

    def of(self, ap):
        if isinstance(self.at, int):
            return ap[self.at]
        part = ap[bass.ds(self.at, 1)]
        names = " ".join("abcdefg"[:len(part.shape) - 2])
        return part.rearrange(f"o p {names} -> (o p) {names}")


def conv_rotate_kernel(nc, x, weight, rota, out):
    tap_lines = nc.dram_tensor("tap_lines", (C, LINE), F32, kind="Internal").ap()
    x1_dram = nc.dram_tensor("x1_scratch", (C, CHUNKS, B, P), F32, kind="Internal").ap()
    norm2_dram = nc.dram_tensor("norm2_scratch", (C, 2 * B), F32, kind="Internal").ap()

    x_src = x.rearrange("b (g c) (i r) w -> g (c i) b (r w)", c=GC, r=ROWS)
    x1_dst = x1_dram.rearrange("(g c) i b e -> g (c i) (b e)", c=GC)
    norm2_dst = norm2_dram.rearrange("(g c) k -> g c k", c=GC)
    x1_src = [x1_dram[:, :, n * BH:(n + 1) * BH, :].rearrange("c (u i) b e -> u c i (b e)", i=UCH) for n in range(2)]
    out_dst = [[out[n * BH:(n + 1) * BH].rearrange("b c (u i r) w -> u i c b (r w)", i=UCH, r=ROWS)[:, i]
                for i in range(UCH)] for n in range(2)]
    rota_src = rota.rearrange("h v c -> v h c")

    with ExitStack() as ctx:
        def sb(name, shape, dt=F32):
            return ctx.enter_context(nc.sbuf_tensor(name, shape, dt))

        def sem(name):
            return ctx.enter_context(nc.semaphore(name))

        tiles = sb("tiles", [P, max(XRING, GRING), B * P])
        g = sb("g", [P, B, P])
        high = sb("high", [P, 2, B, GC, CHUNKS + 2], F32R)
        low = sb("low", [P, 2, B, GC, CHUNKS + 2], F32R)
        y = sb("y", [P, 2, B, GC, CHUNKS])
        taps_raw = sb("taps_raw", [P, 2, GC, 6, PITCH])
        taps_hi = sb("taps_hi", [P, 2, GC, 6, W], F32R)
        taps_lo = sb("taps_lo", [P, 2, GC, 6, W], F32R)
        rot_all = sb("rot_all", [C, H, C])
        line = sb("line", [C, LINE])
        w_sb = sb("w_sb", [C, 9])
        ident = sb("ident", [P, P])
        ones_mean = sb("ones_mean", [P, P])
        eps = sb("eps", [P, 1])
        carrier = sb("carrier", [P, Q])
        warm = sb("warm", [P, 1])
        stats = sb("stats", [P, 2, 2, B, 3])
        dev = sb("dev", [P, 2 * B])
        dev2 = sb("dev2", [P, 2 * B])
        spread = sb("spread", [P, 2 * B])
        std = sb("std", [P, 2, B])
        affine = sb("affine", [P, 2, 2, 2, B])
        norm2 = sb("norm2", [C, 2, B])

        ps = ctx.enter_context(nc.psum_tensor("ps", [P, 8, 512], F32))
        ps_turn = ps[:, 0:2, :]
        ps_conv = ps[:, 2:4, :]
        ps_back = ps[:, 4:6, :]
        ps_mean = ps[:, 6, 0:2 * B]
        ps_var = ps[:, 7, 0:2 * B]

        def flat(t, n, cols):
            return t[:, n].rearrange("p a b c -> p (a b c)")[:, 0:cols]

        gn = [flat(y, n, GCOLS) for n in range(2)]
        gn_hi = [flat(high, n, GCOLS) for n in range(2)]
        gn_lo = [flat(low, n, GCOLS) for n in range(2)]
        def chunk(granule, i):
            return granule[:, i * (GCOLS // UCH):(i + 1) * (GCOLS // UCH)]

        rot_raw = [flat(taps_raw, n, RH * C) for n in range(2)]
        rot_hi = [flat(taps_hi, n, RH * C) for n in range(2)]
        rot_lo = [flat(taps_lo, n, RH * C) for n in range(2)]

        w_landed = sem("w_landed")
        line_zeroed = sem("line_zeroed")
        line_ready = sem("line_ready")
        line_stored = sem("line_stored")
        ident_zeroed = sem("ident_zeroed")
        consts_ready = sem("consts_ready")
        x_landed = [sem(f"x_landed{n}") for n in range(2)]
        taps_landed = [sem(f"taps_landed{n}") for n in range(2)]
        taps_rounded = sem("taps_rounded")
        taps_split = sem("taps_split")
        stats_ready = sem("stats_ready")
        mean_ready = sem("mean_ready")
        dev_ready = sem("dev_ready")
        dev2_ready = sem("dev2_ready")
        spread_ready = sem("spread_ready")
        var_ready = sem("var_ready")
        std_ready = sem("std_ready")
        scale_ready = sem("scale_ready")
        affine_ready = sem("affine_ready")
        normed_pool = sem("normed_pool")
        normed_act = sem("normed_act")
        turned = sem("turned")
        high_ready = sem("high_ready")
        low_ready = sem("low_ready")
        convolved = sem("convolved")
        y_ready = sem("y_ready")
        turned_back = sem("turned_back")
        x1_ready = sem("x1_ready")
        x1_stored = [sem(f"x1_stored{n}") for n in range(2)]
        norm2_stored = [sem(f"norm2_stored{n}") for n in range(2)]
        norm2_landed = sem("norm2_landed")
        x1_landed = [sem(f"x1_landed{n}") for n in range(GRING)]
        rot_landed = sem("rot_landed")
        x1_early = [sem(f"x1_early{n}") for n in range(len(EARLY_STEPS))]
        rot_staged = sem("rot_staged")
        rot_turned = sem("rot_turned")
        rot_high = sem("rot_high")
        rot_split = sem("rot_split")
        gn_ready = sem("gn_ready")
        gn_high = sem("gn_high")
        gn_split = sem("gn_split")
        rotated = sem("rotated")
        out_ready = sem("out_ready")
        out_stored = [sem(f"out_stored{n}") for n in range(GRING)]

        block = ctx.enter_context(nc.Block())

        def has(s, shift):
            return 0 <= s.res + shift < GROUPS

        def norms(s):
            return 0 if has(s, 3) else 1, 2 if has(s, -2) else 1

        def finishes_norms(s):
            return has(s, 3) or has(s, -2)

        def turns(s, q):
            k, quarter = (s + 1, q + 1) if q + 1 < Q else (s + 2, 0)
            return (k, quarter) if has(k, 0) else None

        def normalises(s, q):
            k, quarter = (s + 1, q + 3) if q + 3 < Q else (s + 2, q + 3 - Q)
            return (k, quarter) if has(k, 0) else None

        def stage1(engine, step):
            for s in range(FIRST_STEP, LOOP_START):
                step(Step(s, s))
            with engine.Fori(0, LOOP_TRIPS) as trip:
                for t in range(UNROLL):
                    step(Step(trip * UNROLL + (LOOP_START + t), LOOP_START + t))
            for s in range(LOOP_START + LOOP_TRIPS * UNROLL, LAST_STEP + 1):
                step(Step(s, s))

        def early_channels(n):
            return (EARLY_STEPS[n] - 1) * GC if n < len(EARLY_STEPS) else 0

        def stage2(engine, unit):
            for u in range(ULOOP_START):
                unit(Step(u, u))
            with engine.Fori(0, ULOOP_TRIPS) as trip:
                for t in range(UUNROLL):
                    unit(Step(trip * UUNROLL + (ULOOP_START + t), ULOOP_START + t))
            for u in range(UNITS - UUNROLL, UNITS):
                unit(Step(u, u))

        def granule(u, half):
            return Step(u.at * 2 + half, u.res * 2 + half)

        @block.sync
        def _(sp):
            sp.dma_start(w_sb[:], weight.rearrange("c o a b -> c (o a b)")).then_inc(w_landed, 16)

            def load(k):
                par = k.ring(2)
                if k.res >= 2:
                    sp.wait_ge(x_landed[par], k.landings(2, 32) - 32)
                x_slot = tiles[:, k.ring(XRING), :].rearrange("p (b e) -> p b e", b=B)
                for half in (slice(0, BH), slice(BH, B)):
                    sp.dma_start(x_slot[:, half], k.of(x_src)[:, half]).then_inc(x_landed[par], 16)

            def load_taps(k):
                par = k.ring(2)
                if k.res >= 2:
                    sp.wait_ge(taps_split, k.at - 1)
                for r in range(ROWS):
                    window = bass.AP(tensor=tap_lines.tensor, offset=k.at * (GC * LINE) + r * PITCH,
                                     ap=[[1, W], [LINE, GC], [1, WINDOW]])
                    sp.dma_start(taps_raw[r * W:(r + 1) * W, par].rearrange("p c s w -> p c (s w)"),
                                 window).then_inc(taps_landed[par], 16)

            for k in range(2):
                load(Step(k, k))
            sp.wait_ge(line_ready, len(POS_IDX + NEG_IDX))
            sp.dma_start(tap_lines, line[:]).then_inc(line_stored, 16)
            load(Step(2, 2))
            sp.wait_ge(line_stored, 16)
            load_taps(Step(0, 0))
            load(Step(3, 3))
            load_taps(Step(1, 1))
            for k in range(4, XRING):
                load(Step(k, k))

            def step(s):
                if s.res in EARLY_STEPS:
                    for par in range(2):
                        sp.wait_ge(x1_stored[par], 16 * ((s.at - par) // 2))
                    for n, early in enumerate(EARLY_STEPS):
                        if early == s.at:
                            sp.dma_start(tiles[0:early_channels(n), n, :].rearrange("p (i f) -> p i f", i=UCH),
                                         x1_src[n % 2][n // 2, 0:early_channels(n)]).then_inc(x1_early[n], 16)
                if s.res >= 0 and has(s, 2):
                    load_taps(s + 2)
                if s.res >= XRING - XAHEAD and has(s, XAHEAD):
                    k = s + XAHEAD
                    sp.wait_ge(x1_stored[k.ring(2)], (k + -XRING).landings(2))
                    load(k)
                if has(s, -1):
                    k = s + -1
                    sp.wait_ge(x1_ready, k.at * Q + Q)
                    sp.dma_start(k.of(x1_dst), tiles[:, k.ring(XRING), :]
                                 ).then_inc(x1_stored[k.ring(2)], 16)
                if has(s, -2):
                    k = s + -2
                    sp.wait_ge(affine_ready, s.at + 4)
                    sp.dma_start(k.of(norm2_dst), affine[0:GC, s.ring(2), 1].rearrange("p a b -> p (a b)")
                                 ).then_inc(norm2_stored[k.ring(2)], 16)
                if s.res > GROUPS - XAHEAD - 1 and s.res <= GROUPS - XAHEAD - 1 + ROT_LOADS:
                    n = s.at - (GROUPS - XAHEAD)
                    rows = slice(n * (H // ROT_LOADS), (n + 1) * (H // ROT_LOADS))
                    sp.dma_start(rot_all[:, rows], rota_src[:, rows]).then_inc(rot_landed, 16)

            stage1(sp, step)

            for n in range(2):
                sp.wait_ge(x1_stored[n], 16 * (GROUPS // 2))
                sp.wait_ge(norm2_stored[n], 16 * (GROUPS // 2))
            sp.dma_start(norm2[:], norm2_dram.rearrange("c (a b) -> c a b", a=2)).then_inc(norm2_landed, 16)

            def load_granule(u, half):
                n = granule(u, half)
                slot = n.ring(GRING)
                if n.res >= GRING:
                    sp.wait_ge(out_stored[slot], n.landings(GRING, 16 * UCH) - 16 * UCH)
                first = early_channels(n.res)
                sp.dma_start(tiles[first:, slot, :].rearrange("p (i f) -> p i f", i=UCH), u.of(x1_src[half])[first:]
                             ).then_inc(x1_landed[slot], 16)

            def store_granule(u, half):
                n = granule(u, half)
                slot = n.ring(GRING)
                for i in range(UCH):
                    sp.wait_ge(out_ready, n.at * RH + (i + 1) * ROWS)
                    sp.dma_start(u.of(out_dst[half][i]),
                                 tiles[:, slot, :].rearrange("p (i b e) -> p i b e", i=UCH, b=BH)[:, i]
                                 ).then_inc(out_stored[slot], 16)

            for u in range(GRING // 2):
                for half in range(2):
                    load_granule(Step(u, u), half)

            def unit(u):
                for half in range(2):
                    store_granule(u, half)
                    if GRING // 2 <= u.res + AHEAD // 2 < UNITS:
                        load_granule(u + AHEAD // 2, half)

            stage2(sp, unit)
            for slot in range(GRING):
                sp.wait_ge(out_stored[slot], 16 * UCH * (2 * UNITS // GRING))

        @block.gpsimd
        def _(pool):
            nc.gpsimd.memset(ident[:], 0.0).then_inc(ident_zeroed, 1)
            nc.gpsimd.memset(ones_mean[:], 1.0 / P).then_inc(consts_ready, 1)
            nc.gpsimd.memset(eps[:], EPS).then_inc(consts_ready, 1)
            pool.wait_ge(ident_zeroed, 1)
            nc.gpsimd.affine_select(out=ident[:], in_=ident[:], compare_op=ALU.not_equal, fill=1.0, base=0,
                                    pattern=[[-1, P]], channel_multiplier=1).then_inc(consts_ready, 1)
            for t in (high, low):
                for n in range(2):
                    for end in (0, CHUNKS + 1):
                        nc.gpsimd.memset(t[:, n, :, :, end:end + 1].bitcast(F32), 0.0).then_inc(consts_ready, 1)

            pool.wait_ge(consts_ready, 3)

            def normalise(k, q):
                pool.wait_ge(affine_ready, k.at + 1)
                if k.res >= 1:
                    pool.wait_ge(turned, (k.at - 1) * Q + q + 1)
                nc.gpsimd.tensor_tensor(carrier[:, q:q + 1], eps[:], eps[:], ALU.mult)
                for b in range(q * QB, q * QB + POOL_QB):
                    last = nc.gpsimd.tensor_scalar(g[:, b, :], tiles[:, k.ring(XRING), b * P:(b + 1) * P],
                                                   affine[:, (k + 1).ring(2), 0, 0, b:b + 1],
                                                   affine[:, (k + 1).ring(2), 0, 1, b:b + 1], ALU.mult, ALU.add)
                last.then_inc(normed_pool, 1)

            def split_taps(k):
                par = k.ring(2)
                pool.wait_ge(taps_rounded, k.at + 1)
                nc.gpsimd.tensor_tensor(taps_lo[:, par], taps_raw[:, par, :, ::-1, W - 1::-1],
                                        taps_hi[:, par].bitcast(F32), ALU.subtract).then_inc(taps_split, 1)

            def step(s):
                for q in range(Q):
                    if normalises(s, q):
                        normalise(*normalises(s, q))
                    if q == 1 and has(s, 1):
                        split_taps(s + 1)

            stage1(pool, step)

            def unit(u):
                for half in range(2):
                    n = granule(u, half)
                    buf = n.ring(2)
                    for i in range(UCH):
                        pool.wait_ge(gn_high, n.at * UCH + i + 1)
                        if n.res >= 2 and i == 0:
                            pool.wait_ge(rotated, (n.at - 1) * RH)
                        nc.gpsimd.tensor_tensor(chunk(gn_lo[buf], i), chunk(gn[buf], i),
                                                chunk(gn_hi[buf], i).bitcast(F32),
                                                ALU.subtract).then_inc(gn_split, 1)

            stage2(pool, unit)

        @block.scalar
        def _(act):
            act.wait_ge(consts_ready, 3)
            nc.scalar.activation(warm[:], eps[:], ACT.Sqrt)

            def normalise(k, q):
                act.wait_ge(affine_ready, k.at + 1)
                if k.res >= 1:
                    act.wait_ge(turned, (k.at - 1) * Q + q + 1)
                for b in range(q * QB + POOL_QB, (q + 1) * QB):
                    last = nc.scalar.activation(g[:, b, :], tiles[:, k.ring(XRING), b * P:(b + 1) * P], ACT.Identity,
                                                scale=affine[:, (k + 1).ring(2), 0, 0, b:b + 1],
                                                bias=affine[:, (k + 1).ring(2), 0, 1, b:b + 1])
                last.then_inc(normed_act, 1)

            def round_taps(k):
                par = k.ring(2)
                act.wait_ge(taps_landed[par], k.landings(2, 16 * ROWS))
                if k.res >= 2:
                    act.wait_ge(convolved, (k.at - 1) * GC)
                nc.scalar.activation(taps_hi[:, par], taps_raw[:, par, :, ::-1, W - 1::-1],
                                     ACT.Identity).then_inc(taps_rounded, 1)

            def step(s):
                for q in range(Q):
                    if has(s, 0):
                        act.wait_ge(convolved, s.at * GC + q + 1)
                        if s.res >= 2 and q == 0:
                            act.wait_ge(turned_back, (s.at - 1) * Q)
                        nc.scalar.activation(y[:, s.ring(2), :, q, :],
                                             ps_conv[:, q % 2, :].rearrange("p (b i) -> p b i", b=B),
                                             ACT.Identity).then_inc(y_ready, 1)
                    if turns(s, q):
                        k, t = turns(s, q)
                        act.wait_ge(turned, k.at * Q + t + 1)
                        if k.res >= 2 and t == 0:
                            act.wait_ge(convolved, (k.at - 1) * GC)
                        nc.scalar.activation(
                            high[:, k.ring(2), t * QB:(t + 1) * QB, :, 1:CHUNKS + 1],
                            ps_turn[:, t % 2, :].rearrange("p (b c i) -> p b c i", b=QB, c=GC),
                            ACT.Identity).then_inc(high_ready, 1)
                    if q == 3 and finishes_norms(s):
                        lo, hi = norms(s)
                        act.wait_ge(var_ready, s.at + 4)
                        nc.scalar.activation(std[:, lo:hi, :],
                                             ps_var[:, lo * B:hi * B].rearrange("p (k b) -> p k b", b=B),
                                             ACT.Sqrt, bias=eps[:, 0:1]).then_inc(std_ready, 1)
                    if q == 0 and has(s, 1):
                        round_taps(s + 1)
                    if normalises(s, q):
                        normalise(*normalises(s, q))

            stage1(act, step)

            def stage_rotations(u):
                if u.res >= 2:
                    act.wait_ge(rot_turned, u.at - 1)
                nc.scalar.activation(rot_raw[u.ring(2)].rearrange("v (h c) -> v h c", h=RH),
                                     rot_all[:, u.rows(RH), :], ACT.Identity).then_inc(rot_staged, 1)

            act.wait_ge(rot_landed, 16 * ROT_LOADS)
            act.wait_ge(taps_split, GROUPS)
            stage_rotations(Step(0, 0))
            act.wait_ge(norm2_landed, 16)

            def unit(u):
                if u.res + 1 < UNITS:
                    stage_rotations(u + 1)
                for half in range(2):
                    n = granule(u, half)
                    slot, buf = n.ring(GRING), n.ring(2)
                    act.wait_ge(x1_landed[slot], n.landings(GRING))
                    if n.res < len(EARLY_STEPS):
                        act.wait_ge(x1_early[n.res], 16)
                    if n.res >= 2:
                        act.wait_ge(gn_split, (n.at - 1) * UCH)
                    src = tiles[:, slot, :].rearrange("p (i b e) -> p i b e", i=UCH, b=BH)
                    dst = gn[buf].rearrange("p (i b e) -> p i b e", i=UCH, b=BH)
                    for b in range(BH):
                        image = half * BH + b
                        last = nc.scalar.activation(dst[:, :, b, :], src[:, :, b, :], ACT.Identity,
                                                    scale=norm2[:, 0, image:image + 1],
                                                    bias=norm2[:, 1, image:image + 1])
                    last.then_inc(gn_ready, 1)
                    if half == 0:
                        act.wait_ge(rot_turned, u.at + 1)
                        if u.res >= 2:
                            act.wait_ge(rotated, (u.at - 1) * 2 * RH)
                        nc.scalar.activation(rot_hi[u.ring(2)], ps[:, 0, :], ACT.Identity).then_inc(rot_high, 1)

            stage2(act, unit)

        @block.vector
        def _(dve):
            nc.vector.memset(line[:], 0.0).then_inc(line_zeroed, 1)
            dve.wait_ge(line_zeroed, 1)
            dve.wait_ge(w_landed, 16)
            for places, sign in ((POS_IDX, 1.0), (NEG_IDX, -1.0)):
                for tap, place in enumerate(places):
                    dy, dx = place // KW - KH // 2, place % KW - KW // 2
                    at = (dy + 3) * PITCH + SLOT_MID + dx
                    nc.vector.tensor_scalar(line[:, at:at + 1], w_sb[:, tap + 1:tap + 2], sign, None,
                                            ALU.mult).then_inc(line_ready, 1)

            def step(s):
                now, later = s.ring(2), (s + 1).ring(2)
                lo, hi = norms(s)
                cols = slice(lo * B, hi * B)

                def statistics(norm, tile, q):
                    for b in range(q * QB, (q + 1) * QB, 2):
                        last = nc.vector.bn_stats(out=stats[:, later, norm, b:b + 2, :].rearrange("p b f -> p (b f)"),
                                                  in_=tile[:, b * P:(b + 2) * P].rearrange("p (b e) -> p e b", b=2))
                    return last

                for q in range(Q):
                    if turns(s, q):
                        k, t = turns(s, q)
                        quarter = slice(t * QB, (t + 1) * QB)
                        dve.wait_ge(high_ready, k.at * Q + t + 1)
                        nc.vector.tensor_tensor(
                            low[:, k.ring(2), quarter, :, 1:CHUNKS + 1],
                            ps_turn[:, t % 2, :].rearrange("p (b c i) -> p b c i", b=QB, c=GC),
                            high[:, k.ring(2), quarter, :, 1:CHUNKS + 1].bitcast(F32),
                            ALU.subtract).then_inc(low_ready, 1)
                    if has(s, -1):
                        k = s + -1
                        dve.wait_ge(turned_back, k.at * Q + q + 1)
                        quarter = slice(q * QB * P, (q + 1) * QB * P)
                        x_part = tiles[:, k.ring(XRING), quarter]
                        nc.vector.tensor_tensor(x_part, ps_back[:, q % 2, :], x_part, ALU.add).then_inc(x1_ready, 1)
                    if q == 1 and finishes_norms(s):
                        dve.wait_ge(mean_ready, s.at + 4)
                        nc.vector.tensor_tensor(
                            dev[:, cols], stats[:, now].rearrange("p k b f -> p (k b) f")[:, cols, 1],
                            ps_mean[:, cols], ALU.subtract).then_inc(dev_ready, 1)
                    if q == 0 and finishes_norms(s + -1):
                        dve.wait_ge(var_ready, s.at + 3)
                    if has(s, 4):
                        k = s + 4
                        if q == 0:
                            dve.wait_ge(x_landed[k.ring(2)], k.landings(2, 32))
                        last = statistics(0, tiles[:, k.ring(XRING)], q)
                    if q == 1 and finishes_norms(s):
                        dve.wait_ge(dev_ready, s.at + 4)
                        nc.vector.tensor_tensor(dev2[:, cols], dev[:, cols], dev[:, cols],
                                                ALU.mult).then_inc(dev2_ready, 1)
                    if has(s, -1):
                        k = s + -1
                        dve.wait_ge(x1_ready, k.at * Q + q + 1)
                        last = statistics(1, tiles[:, k.ring(XRING)], q)
                    if q == 1 and finishes_norms(s):
                        dve.wait_ge(dev2_ready, s.at + 4)
                        nc.vector.scalar_tensor_tensor(
                            out=spread[:, cols], in0=stats[:, now].rearrange("p k b f -> p (k b) f")[:, cols, 2],
                            scalar=1.0 / P, in1=dev2[:, cols], op0=ALU.mult, op1=ALU.add).then_inc(spread_ready, 1)
                if has(s, 4) or has(s, -1):
                    last.then_inc(stats_ready, 1)
                if finishes_norms(s):
                    dve.wait_ge(std_ready, s.at + 4)
                    if has(s, 1):
                        dve.wait_ge(normed_pool, s.at * Q + 2 * Q)
                        dve.wait_ge(normed_act, s.at * Q + 2 * Q)
                    if has(s, -3):
                        dve.wait_ge(norm2_stored[later], (s + -3).landings(2))
                    nc.vector.reciprocal(affine[:, now, lo:hi, 0, :], std[:, lo:hi, :]).then_inc(scale_ready, 1)
                    dve.wait_ge(scale_ready, s.at + 4)
                    nc.vector.scalar_tensor_tensor(
                        out=affine[:, now, lo:hi, 1, :],
                        in0=ps_mean[:, cols].rearrange("p (k b) -> p k b", b=B), scalar=-1.0,
                        in1=affine[:, now, lo:hi, 0, :], op0=ALU.mult, op1=ALU.mult).then_inc(affine_ready, 1)

            stage1(dve, step)

            def add_rows(u, half):
                n = granule(u, half)
                dst = tiles[:, n.ring(GRING), :].rearrange("p (i b r w) -> p i b r w", i=UCH, b=BH, r=ROWS)
                for h in range(RH):
                    dve.wait_ge(rotated, n.at * RH + h + 1)
                    xrow = dst[:, h // ROWS, :, h % ROWS, :]
                    nc.vector.tensor_tensor(
                        xrow, ps[:, n.ring(2) * RH + h, :].rearrange("p (b w) -> p b w", b=BH), xrow,
                        ALU.add).then_inc(out_ready, 1)

            def unit(u):
                for half in range(2):
                    n = granule(u, half)
                    dve.wait_ge(gn_ready, n.at + 1)
                    if n.res >= 2:
                        dve.wait_ge(rotated, (n.at - 1) * RH)
                    for i in range(UCH):
                        nc.vector.tensor_copy(chunk(gn_hi[n.ring(2)], i), chunk(gn[n.ring(2)], i)
                                              ).then_inc(gn_high, 1)
                    if half == 1:
                        add_rows(u, 0)
                        continue
                    if u.res >= 1:
                        add_rows(u + -1, 1)
                    dve.wait_ge(rot_high, u.at + 1)
                    nc.vector.tensor_tensor(rot_lo[u.ring(2)], ps[:, 0, :], rot_hi[u.ring(2)].bitcast(F32),
                                            ALU.subtract).then_inc(rot_split, 1)

            stage2(dve, unit)
            add_rows(Step(UNITS - 1, UNITS - 1), 1)

        @block.tensor
        def _(pe):
            pe.wait_ge(consts_ready, 11)

            def products(dst, pairs):
                for n, (weights, moving) in enumerate(pairs):
                    last = nc.tensor.matmul(dst, weights, moving, start=(n == 0), stop=(n == len(pairs) - 1))
                return last

            def convolve(s, c):
                par = s.ring(2)
                if c == 0:
                    pe.wait_ge(low_ready, s.at * Q + Q)
                    pe.wait_ge(taps_split, s.at + 1)
                if s.res >= 1 or c >= 2:
                    pe.wait_ge(y_ready, s.at * GC + c - 1)
                pairs = []
                for j in (0, -1, 1):
                    slots = slice(2 * (1 - j), 2 * (1 - j) + 2)
                    hi_w = taps_hi[:, par, c, slots, :].rearrange("p s w -> p (s w)")
                    lo_w = taps_lo[:, par, c, slots, :].rearrange("p s w -> p (s w)")
                    hi_x = high[:, par, :, c, 1 + j:1 + j + CHUNKS]
                    lo_x = low[:, par, :, c, 1 + j:1 + j + CHUNKS]
                    pairs += [(hi_w, hi_x), (hi_w, lo_x), (lo_w, hi_x)]
                products(ps_conv[:, c % 2, :], pairs).then_inc(convolved, 1)

            def turn(k, q):
                pe.wait_ge(normed_pool, k.at * Q + q + 1)
                pe.wait_ge(normed_act, k.at * Q + q + 1)
                if k.res >= 1 or q >= 2:
                    pe.wait_ge(low_ready, k.at * Q + q - 1)
                for n in range(QB):
                    last = nc.tensor.transpose(ps_turn[:, q % 2, n * P:(n + 1) * P], g[:, q * QB + n, :], ident[:])
                last.then_inc(turned, 1)

            def turn_back(k, q):
                if q == 0:
                    pe.wait_ge(y_ready, k.at * GC + GC)
                if k.res >= 1 or q >= 2:
                    pe.wait_ge(x1_ready, k.at * Q + q - 1)
                for n in range(QB):
                    last = nc.tensor.transpose(ps_back[:, q % 2, n * P:(n + 1) * P],
                                               y[:, k.ring(2), q * QB + n].rearrange("p c i -> p (c i)"), ident[:])
                last.then_inc(turned_back, 1)

            def step(s):
                for q in range(Q):
                    if has(s, 0):
                        convolve(s, q)
                    if finishes_norms(s) and q in (1, 3):
                        lo, hi = norms(s)
                        cols = slice(lo * B, hi * B)
                        field = stats[:, s.ring(2)].rearrange("p k b f -> p (k b) f")
                        if q == 1:
                            pe.wait_ge(stats_ready, s.at + 4)
                            if finishes_norms(s + -1):
                                pe.wait_ge(affine_ready, s.at + 3)
                            products(ps_mean[:, cols], [(ones_mean[:], field[:, cols, 1])]).then_inc(mean_ready, 1)
                        else:
                            pe.wait_ge(spread_ready, s.at + 4)
                            products(ps_var[:, cols], [(ones_mean[:], spread[:, cols])]).then_inc(var_ready, 1)
                    if turns(s, q):
                        turn(*turns(s, q))
                    if has(s, -1):
                        turn_back(s + -1, q)

            stage1(pe, step)

            def turn_rotations(u):
                par = u.ring(2)
                pe.wait_ge(rot_staged, u.at + 1)
                if u.res >= 1:
                    pe.wait_ge(out_ready, (u.at - 1) * 2 * RH + 1)
                    pe.wait_ge(rot_split, u.at)
                for h in range(RH):
                    last = nc.tensor.transpose(ps[:, 0, h * P:(h + 1) * P], rot_raw[par][:, h * C:(h + 1) * C],
                                               ident[:])
                last.then_inc(rot_turned, 1)

            turn_rotations(Step(0, 0))

            def unit(u):
                pe.wait_ge(rot_split, u.at + 1)
                par = u.ring(2)
                for half in range(2):
                    n = granule(u, half)
                    buf = n.ring(2)
                    hi_x = gn_hi[buf].rearrange("p (i b r w) -> p i b r w", i=UCH, b=BH, r=ROWS)
                    lo_x = gn_lo[buf].rearrange("p (i b r w) -> p i b r w", i=UCH, b=BH, r=ROWS)
                    for h in range(RH):
                        if h % ROWS == 0:
                            pe.wait_ge(gn_split, n.at * UCH + h // ROWS + 1)
                        if n.res >= 2:
                            pe.wait_ge(out_ready, (n.at - 2) * RH + h + 1)
                        hi_w, lo_w = (t[par][:, h * P:(h + 1) * P] for t in (rot_hi, rot_lo))
                        at = (h // ROWS, slice(None), h % ROWS)
                        products(ps[:, n.ring(2) * RH + h, :],
                                 [(hi_w, hi_x[:, at[0], :, at[2], :]), (hi_w, lo_x[:, at[0], :, at[2], :]),
                                  (lo_w, hi_x[:, at[0], :, at[2], :])]).then_inc(rotated, 1)
                    if half == 0 and u.res + 1 < UNITS:
                        turn_rotations(u + 1)

            stage2(pe, unit)


_INS = ['x', 'L0_conv_weight', 'L1_conv_rota_matrix']
_OUTS = [((B, C, H, W), 'float32')]


def kernel(**inputs):
    import numpy as _np
    import concourse.bacc as _bacc
    from concourse import mybir as _mybir
    from concourse.bass_utils import run_bass_kernel_spmd as _run

    nc = _bacc.Bacc("TRN2", target_bir_lowering=False, num_devices=1)
    arrays, args = {}, []
    for name in _INS:
        a = _np.ascontiguousarray(inputs[name])
        arrays[f"in_{name}_dram"] = a
        args.append(nc.dram_tensor(f"in_{name}_dram", a.shape, _mybir.dt.from_np(a.dtype), kind="ExternalInput").ap())
    for i, (shape, dtype) in enumerate(_OUTS):
        dt = _mybir.dt.from_np(_np.dtype(dtype))
        args.append(nc.dram_tensor(f"out_{i}_dram", shape, dt, kind="ExternalOutput").ap())
    conv_rotate_kernel(nc, *args)
    r = _run(nc, [arrays], core_ids=[0])
    got = tuple(r.results[0][f"out_{i}_dram"] for i in range(len(_OUTS)))
    return got[0]
```
